# Optimizing a Trainium2 kernel written in Bass

```python
import numpy as np
import jax
import jax.numpy as jnp

def _softmax(x, axis=-1):
    return jax.nn.softmax(x, axis=axis)

def _gelu(x):
    return jax.nn.gelu(x, approximate=True)

def _silu(x):
    return jax.nn.silu(x)

def _sigmoid(x):
    return jax.nn.sigmoid(x)

def _layernorm(x, axis=-1, eps=1e-05):
    m = jnp.mean(x, axis=axis, keepdims=True)
    v = jnp.var(x, axis=axis, keepdims=True)
    return (x - m) / jnp.sqrt(v + eps)

def _scatter_add(tgt, idx, src, axis=0):
    return tgt.at[idx].add(src)

def _segment_sum(src, seg, n):
    return jax.ops.segment_sum(src, seg, n)
kernel_name = 'mk_adj_resnorm_d1_adj_r2_e5d22d'

def setup_inputs(seed: int=0):
    np.random.seed(seed)
    _w = jnp.asarray

    def _rec_inputs():
        import jax
        import jax.numpy as jnp
        _gk = jax.random.key(seed)
        x = 0.0002141 + 1 * jax.random.normal(jax.random.fold_in(_gk, 1), (128, 64, 384), jnp.float32)
        _a = jax.random.bernoulli(jax.random.fold_in(_gk, 2), 0.125, (128, 64, 64))
        _a = jnp.logical_or(_a, jnp.swapaxes(_a, -1, -2))
        _a = jnp.logical_or(_a, jnp.eye(64, dtype=bool))
        adj = _a.astype(jnp.int32)
        return (x, adj)
    x, adj = _rec_inputs()

    def _L0_gnn_setup():
        import jax, jax.numpy as jnp
        import numpy as np
        B, S, HID, DEP, DS, NTYPES = (8, 128, 384, 64, 384, 45)
        NEG = -1000000000.0
        key = jax.random.key(seed)
        ks = jax.random.split(key, 10)
        sc = lambda fan_in: 1.0 / np.sqrt(fan_in)
        return {'h': jax.random.normal(ks[0], (B, S, HID), dtype=jnp.float32), 'dep_type_matrix': jax.random.randint(ks[1], (B, S, S), 0, NTYPES), 'dep_emb_table': jax.random.normal(ks[2], (NTYPES, DEP), dtype=jnp.float32), 'W1_w': jax.random.normal(ks[3], (HID + DEP, DS), dtype=jnp.float32) * sc(HID + DEP), 'W1_b': jnp.zeros((DS,), dtype=jnp.float32), 'W2_w': jax.random.normal(ks[4], (HID + DEP, DS), dtype=jnp.float32) * sc(HID + DEP), 'W2_b': jnp.zeros((DS,), dtype=jnp.float32), 'gcn_w': jax.random.normal(ks[5], (HID, HID), dtype=jnp.float32) * sc(HID), 'gcn_b': jnp.zeros((HID,), dtype=jnp.float32), 'Wo_w': jax.random.normal(ks[6], (DS, HID), dtype=jnp.float32) * sc(DS), 'Wo_b': jnp.zeros((HID,), dtype=jnp.float32)}
    _L0_gnn_all = _L0_gnn_setup()
    _L0_gnn_in = {k: v for k, v in _L0_gnn_all.items() if k in ('dep_emb_table', 'W1_w', 'W1_b', 'W2_w', 'W2_b', 'gcn_w', 'gcn_b', 'Wo_w', 'Wo_b')}
    del _L0_gnn_all
    return {'x': x, 'adj': adj, 'L0_gnn_dep_emb_table': _L0_gnn_in['dep_emb_table'], 'L0_gnn_W1_w': _L0_gnn_in['W1_w'], 'L0_gnn_W1_b': _L0_gnn_in['W1_b'], 'L0_gnn_W2_w': _L0_gnn_in['W2_w'], 'L0_gnn_W2_b': _L0_gnn_in['W2_b'], 'L0_gnn_gcn_w': _L0_gnn_in['gcn_w'], 'L0_gnn_gcn_b': _L0_gnn_in['gcn_b'], 'L0_gnn_Wo_w': _L0_gnn_in['Wo_w'], 'L0_gnn_Wo_b': _L0_gnn_in['Wo_b']}

def reference(x, adj, L0_gnn_dep_emb_table, L0_gnn_W1_w, L0_gnn_W1_b, L0_gnn_W2_w, L0_gnn_W2_b, L0_gnn_gcn_w, L0_gnn_gcn_b, L0_gnn_Wo_w, L0_gnn_Wo_b):
    import jax
    import jax.numpy as jnp

    def _L0_gnn_ref(h, dep_type_matrix, dep_emb_table, W1_w, W1_b, W2_w, W2_b, gcn_w, gcn_b, Wo_w, Wo_b):
        import jax, jax.numpy as jnp
        import numpy as np
        B, S, HID, DEP, DS, NTYPES = (8, 128, 384, 64, 384, 45)
        NEG = -1000000000.0
        adj = dep_type_matrix != 0
        dep_emb = dep_emb_table[dep_type_matrix]
        hi_t = jnp.einsum('bid,de->bie', h, W1_w[:HID])[:, :, None, :] + jnp.einsum('bijd,de->bije', dep_emb, W1_w[HID:]) + W1_b
        hj_t = jnp.einsum('bjd,de->bje', h, W2_w[:HID])[:, None, :, :] + jnp.einsum('bijd,de->bije', dep_emb, W2_w[HID:]) + W2_b
        relevance = jnp.sum(hi_t * hj_t, axis=-1)
        masked = jnp.where(adj, relevance, NEG)
        A = jax.nn.softmax(masked, axis=2)
        h_syn = h
        for _ in range(1):
            aggregated = jnp.einsum('bij,bjd->bid', A, h_syn)
            h_syn = jax.nn.relu(aggregated @ gcn_w + gcn_b)
        return h_syn @ Wo_w + Wo_b
    x = _layernorm(x + _L0_gnn_ref(x, adj, L0_gnn_dep_emb_table, L0_gnn_W1_w, L0_gnn_W1_b, L0_gnn_W2_w, L0_gnn_W2_b, L0_gnn_gcn_w, L0_gnn_gcn_b, L0_gnn_Wo_w, L0_gnn_Wo_b), axis=-1)
    return x

_drawn_inputs = setup_inputs


def setup_inputs(seed=0):
    import zlib

    import numpy as np

    out = dict(_drawn_inputs(seed))
    spreads = {'L0_gnn_W1_b': (0.0, 0.1),
     'L0_gnn_W2_b': (0.0, 0.1),
     'L0_gnn_gcn_b': (0.0, 0.1),
     'L0_gnn_Wo_b': (0.0, 0.1)}
    factors = {}
    for name, (base, spread) in spreads.items():
        noise = np.random.default_rng([zlib.crc32(name.encode()), seed]).standard_normal(out[name].shape)
        drawn = base * np.exp(spread * noise) if base else spread * noise
        out[name] = jnp.asarray(drawn.astype(out[name].dtype))
    for name, factor in factors.items():
        out[name] = (out[name] * factor).astype(out[name].dtype)
    return out
```

```python
from contextlib import ExitStack

import concourse.bass as bass
from concourse import mybir

F32 = mybir.dt.float32
F32R = mybir.dt.float32r
I32 = mybir.dt.int32
ALU = mybir.AluOpType
ACT = mybir.ActivationFunctionType
AX_X = mybir.AxisListType.X

P = 128
NEG = 1.0e9
EPS = 1e-5


def gnn_layernorm_kernel(nc, x, x_t, adj, emb_t, w1_t, w1_e, w1_b, w2_t, w2_e, w2_b,
                         gcn_w, gcn_b, wo_w, wo_b, out):
    HID, TOKENS = x_t.shape
    NODES = adj.shape[2]
    EDIM, NTYPES = emb_t.shape
    C = HID // P
    PAIRS = 4
    GT = PAIRS * P
    GROUPS = TOKENS // GT
    HW = HID + 2
    assert 2 * NODES == P and GROUPS % 2 == 0 and GROUPS >= 4

    x_rows = x.rearrange("b n d -> (b n) d").rearrange("(g q p) d -> g p q d", q=PAIRS, p=P)
    out_rows = out.rearrange("b n d -> (b n) d").rearrange("(g q p) d -> g p q d", q=PAIRS, p=P)
    xt_cols = x_t.rearrange("(c p) (g t) -> g p c t", p=P, t=GT)
    adj_rows = adj.rearrange("b i j -> (b i) j").rearrange("(g q p) j -> g p q j", q=PAIRS, p=P)

    with ExitStack() as ctx:
        def sb(name, shape, dt=F32):
            return ctx.enter_context(nc.sbuf_tensor(name, shape, dt))

        def sem(name):
            return ctx.enter_context(nc.semaphore(name))

        ident = sb("ident", [P, P])
        w1t_sb = sb("w1t_sb", [P, C, HID])
        w2t_sb = sb("w2t_sb", [P, C, HID])
        w1e_sb = sb("w1e_sb", [EDIM, HID])
        w2e_sb = sb("w2e_sb", [EDIM, HID])
        emb_sb = sb("emb_sb", [EDIM, NTYPES])
        b1_sb = sb("b1_sb", [P, C])
        b2_sb = sb("b2_sb", [P, C])
        gb_sb = sb("gb_sb", [P, C])
        wob_sb = sb("wob_sb", [P, HID])
        gcn_sb = sb("gcn_sb", [P, C, HID])
        wo_sb = sb("wo_sb", [P, C, HID])
        c1_sb = sb("c1_sb", [P, C])
        c2_sb = sb("c2_sb", [P, C])
        r_sb = sb("r_sb", [P, C])
        k_sb = sb("k_sb", [P, 1])
        m_hi = sb("m_hi", [P, C, HID], F32R)
        m_lo = sb("m_lo", [P, C, HID], F32R)
        gcn_hi = sb("gcn_hi", [P, C, HW], F32R)
        gcn_lo = sb("gcn_lo", [P, C, HW], F32R)
        wo_hi = sb("wo_hi", [P, C, HID], F32R)
        wo_lo = sb("wo_lo", [P, C, HID], F32R)
        xt_sb = sb("xt_sb", [P, 2, C, GT])
        xt_hi = sb("xt_hi", [P, 2, C, GT], F32R)
        xt_lo = sb("xt_lo", [P, 2, C, GT], F32R)
        x_sb = sb("x_sb", [P, 2, PAIRS, HID])
        adj_sb = sb("adj_sb", [P, 2, PAIRS, NODES], I32)
        neg_sb = sb("neg_sb", [P, 2, PAIRS, NODES])
        g_hi = sb("g_hi", [P, C, GT], F32R)
        g_lo = sb("g_lo", [P, C, GT], F32R)
        hg_hi = sb("hg_hi", [P, 2, PAIRS, HID], F32R)
        hg_lo = sb("hg_lo", [P, 2, PAIRS, HID], F32R)
        srow = sb("srow", [P, 2, PAIRS])
        rel = sb("rel", [P, PAIRS, NODES])
        nmax = sb("nmax", [P, PAIRS])
        prob = sb("prob", [P, PAIRS, NODES])
        psum_row = sb("psum_row", [P, PAIRS])
        rsum = sb("rsum", [P, PAIRS])
        attn = sb("attn", [P, PAIRS, P])
        at_hi = sb("at_hi", [P, GT], F32R)
        at_lo = sb("at_lo", [P, GT], F32R)
        hs_sb = sb("hs_sb", [P, C, GT])
        hs_hi = sb("hs_hi", [P, C, GT], F32R)
        hs_lo = sb("hs_lo", [P, C, GT], F32R)
        y_sb = sb("y_sb", [P, 2, PAIRS, HID])
        stats = sb("stats", [P, PAIRS, 6])
        mv = sb("mv", [P, PAIRS, 2])
        veps = sb("veps", [P, PAIRS])
        mhalf = sb("mhalf", [P, PAIRS])
        eps_sb = sb("eps_sb", [P, PAIRS])
        rstd = sb("rstd", [P, PAIRS])
        nmr = sb("nmr", [P, PAIRS])

        bank = [ctx.enter_context(nc.psum_tensor(f"bank{i}", [P, 512], F32)) for i in range(8)]
        PROJ_BANK = bank[0:3]
        OUT_BANK = bank[3:7]
        VALUE_BANK = bank[0:4]
        MIX_BANK = bank[4:7]
        score = bank[7]

        w12_loaded = sem("w12_loaded")
        small_loaded = sem("small_loaded")
        gcn_loaded = sem("gcn_loaded")
        wo_loaded = sem("wo_loaded")
        xt_loaded = [sem(f"xt_loaded{i}") for i in range(2)]
        x_loaded = [sem(f"x_loaded{i}") for i in range(2)]
        adj_loaded = [sem(f"adj_loaded{i}") for i in range(2)]
        stored = [sem(f"stored{i}") for i in range(2)]
        ident_zero = sem("ident_zero")
        ident_ready = sem("ident_ready")
        attn_zero = sem("attn_zero")
        c_mm = sem("c_mm")
        c_ready = sem("c_ready")
        m_mm = sem("m_mm")
        m_hi_ready = sem("m_hi_ready")
        m_lo_ready = sem("m_lo_ready")
        ruk_mm = sem("ruk_mm")
        u_hi_ready = sem("u_hi_ready")
        ruk_ready = sem("ruk_ready")
        w_hi_ready = sem("w_hi_ready")
        w_lo_ready = sem("w_lo_ready")
        xhi = sem("xhi")
        xlo = sem("xlo")
        negm = sem("negm")
        xb = sem("xb")
        proj_mm = sem("proj_mm")
        ghi = sem("ghi")
        glo = sem("glo")
        score_mm = sem("score_mm")
        value_mm = sem("value_mm")
        hghi = sem("hghi")
        hglo = sem("hglo")
        masked = sem("masked")
        expd = sem("expd")
        normed = sem("normed")
        turn_mm = sem("turn_mm")
        athi = sem("athi")
        atlo = sem("atlo")
        mix_mm = sem("mix_mm")
        hsr = sem("hsr")
        hshi = sem("hshi")
        hslo = sem("hslo")
        out_mm = sem("out_mm")
        added = sem("added")
        statd = sem("statd")
        aggrd = sem("aggrd")
        veps_ready = sem("veps_ready")
        rstd_ready = sem("rstd_ready")
        nmr_ready = sem("nmr_ready")
        y_ready = sem("y_ready")

        def f32(ap):
            return ap.bitcast(F32)

        def run(eng, body):
            body(0, 0, True, False)
            with eng.Fori(0, (GROUPS - 2) // 2) as i:
                body(2 * i + 1, 1, False, False)
                body(2 * i + 2, 0, False, False)
            body(GROUPS - 1, 1, False, True)

        def half(g, slot):
            return g // 2 if isinstance(g, int) else (g - slot) // 2

        block = ctx.enter_context(nc.Block())

        @block.sync
        def _(sp):
            sp.dma_start(w1t_sb[:], w1_t.rearrange("(c p) n -> p c n", p=P)).then_inc(w12_loaded, 16)
            sp.dma_start(w2t_sb[:], w2_t.rearrange("(c p) n -> p c n", p=P)).then_inc(w12_loaded, 16)
            sp.dma_start(xt_sb[:, 0], xt_cols[0]).then_inc(xt_loaded[0], 16)
            sp.dma_start(gcn_sb[:], gcn_w.rearrange("(c p) n -> p c n", p=P)).then_inc(gcn_loaded, 16)
            sp.dma_start(adj_sb[:, 0], adj_rows[0]).then_inc(adj_loaded[0], 16)
            sp.dma_start(xt_sb[:, 1], xt_cols[1]).then_inc(xt_loaded[1], 16)
            sp.dma_start(wo_sb[:], wo_w.rearrange("(c p) n -> p c n", p=P)).then_inc(wo_loaded, 16)
            sp.dma_start(adj_sb[:, 1], adj_rows[1]).then_inc(adj_loaded[1], 16)
            sp.dma_start(x_sb[:, 0], x_rows[0]).then_inc(x_loaded[0], 16)

            def body(g, par, first, last):
                if not last:
                    if not first:
                        sp.wait_ge(added, PAIRS * g)
                    sp.dma_start(x_sb[:, 1 - par], x_rows[g + 1]).then_inc(x_loaded[1 - par], 16)
                if not first:
                    sp.wait_ge(y_ready, g)
                    sp.dma_start(out_rows[g - 1], y_sb[:, 1 - par]).then_inc(stored[1 - par], 16)

            body(0, 0, True, False)
            with sp.Fori(0, (GROUPS - 2) // 2) as i:
                for par in (1, 0):
                    g = 2 * i + 2 - par
                    sp.wait_ge(xlo, g)
                    sp.dma_start(xt_sb[:, 1 - par], xt_cols[g + 1]).then_inc(xt_loaded[1 - par], 16)
                    sp.wait_ge(masked, 3 * g)
                    sp.dma_start(adj_sb[:, 1 - par], adj_rows[g + 1]).then_inc(adj_loaded[1 - par], 16)
                    body(g, par, False, False)
            body(GROUPS - 1, 1, False, True)
            sp.wait_ge(y_ready, GROUPS)
            sp.dma_start(out_rows[GROUPS - 1], y_sb[:, 1]).then_inc(stored[1], 16)
            for slot in range(2):
                sp.wait_ge(stored[slot], 16 * (GROUPS // 2))

        @block.tensor
        def _(pe):
            def three(acc, a_hi, a_lo, b_hi, b_lo, first, last):
                pe.matmul(acc, a_hi, b_hi, start=first, stop=False)
                pe.matmul(acc, a_hi, b_lo, start=False, stop=False)
                return pe.matmul(acc, a_lo, b_hi, start=False, stop=last)

            def proj(g, par):
                pe.wait_ge(xlo, g + 1)
                for f in range(C):
                    pe.wait_ge(hglo, PAIRS * g + f + 1)
                    fs = slice(f * P, (f + 1) * P)
                    for c in range(C):
                        mm = three(PROJ_BANK[f][:, 0:GT], m_hi[:, c, fs], m_lo[:, c, fs],
                                   xt_hi[:, par, c, :], xt_lo[:, par, c, :], c == 0, c == C - 1)
                    mm.then_inc(proj_mm, 1)

            def score_stage(g, par):
                pe.wait_ge(glo, C * (g + 1))
                if not (isinstance(g, int) and g == 0):
                    pe.wait_ge(atlo, g)
                for q in range(PAIRS):
                    ts = slice(q * P, (q + 1) * P)
                    for c in range(C):
                        mm = three(score[:, ts], g_hi[:, c, ts], g_lo[:, c, ts],
                                   xt_hi[:, par, c, ts], xt_lo[:, par, c, ts], c == 0, c == C - 1)
                mm.then_inc(score_mm, 1)

            def value(g, par, q):
                pe.wait_ge(xlo, g + 1)
                if not isinstance(g, int) or g > 0:
                    if q < C:
                        pe.wait_ge(glo, C * (g - 1) + q + 1)
                    elif not isinstance(g, int) or g > 1:
                        pe.wait_ge(added, PAIRS * (g - 2) + 1)
                ts = slice(q * P, (q + 1) * P)
                for c in range(C):
                    mm = three(VALUE_BANK[q][:, 0:HW], xt_hi[:, par, c, ts], xt_lo[:, par, c, ts],
                               gcn_hi[:, c, :], gcn_lo[:, c, :], c == 0, c == C - 1)
                mm.then_inc(value_mm, 1)

            def turn(g):
                pe.wait_ge(normed, 2 * (g + 1))
                for q in range(PAIRS):
                    mm = pe.transpose(score[:, q * P:(q + 1) * P], attn[:, q, :], ident[:])
                mm.then_inc(turn_mm, 1)

            def mix(g, par):
                pe.wait_ge(atlo, g + 1)
                pe.wait_ge(hglo, PAIRS * (g + 1))
                for f in range(C):
                    if not (isinstance(g, int) and g == 0):
                        pe.wait_ge(added, PAIRS * (g - 1) + f + 2)
                    fs = slice(f * P, (f + 1) * P)
                    for q in range(PAIRS):
                        ts = slice(q * P, (q + 1) * P)
                        mm = three(MIX_BANK[f][:, ts], hg_hi[:, par, q, fs], hg_lo[:, par, q, fs],
                                   at_hi[:, ts], at_lo[:, ts], True, True)
                    mm.then_inc(mix_mm, 1)

            def out_stage(g, q):
                pe.wait_ge(hslo, C * (g + 1))
                if q == 0:
                    if not isinstance(g, int) or g < GROUPS - 1:
                        pe.wait_ge(hglo, PAIRS * (g + 1) + PAIRS)
                else:
                    pe.wait_ge(hsr, C * g + q)
                ts = slice(q * P, (q + 1) * P)
                for c in range(C):
                    mm = three(OUT_BANK[q][:, 0:HID], hs_hi[:, c, ts], hs_lo[:, c, ts],
                               wo_hi[:, c, :], wo_lo[:, c, :], c == 0, c == C - 1)
                mm.then_inc(out_mm, 1)

            pe.wait_ge(small_loaded, 16 * 7)
            for n, w in enumerate((w1e_sb, w2e_sb)):
                for c in range(C):
                    mm = pe.matmul(bank[4][:, n * C + c:n * C + c + 1], w[:, c * P:(c + 1) * P], emb_sb[:, 1:2],
                                   start=True, stop=True)
            mm.then_inc(c_mm, 1)
            pe.wait_ge(w12_loaded, 32)
            for d in range(C):
                for c in range(C):
                    mm = pe.matmul(bank[d][:, 0:HID], w1t_sb[:, c, d * P:(d + 1) * P], w2t_sb[:, c, :],
                                   start=(c == 0), stop=(c == C - 1))
                mm.then_inc(m_mm, 1)
            pe.wait_ge(c_ready, 2)
            for n, (w, v) in enumerate(((w2t_sb, c1_sb), (w1t_sb, c2_sb))):
                for d in range(C):
                    for c in range(C):
                        pe.matmul(bank[5][:, n * C + d:n * C + d + 1], w[:, c, d * P:(d + 1) * P], v[:, c:c + 1],
                                  start=(c == 0), stop=(c == C - 1))
            for c in range(C):
                mm = pe.matmul(bank[5][:, 2 * C:2 * C + 1], c1_sb[:, c:c + 1].to_broadcast([P, P]),
                               c2_sb[:, c:c + 1], start=(c == 0), stop=(c == C - 1))
            mm.then_inc(ruk_mm, 1)

            pe.wait_ge(w_lo_ready, 1)
            pe.wait_ge(ruk_ready, 1)
            pe.wait_ge(m_lo_ready, C)
            pe.wait_ge(ident_ready, 1)
            for q in range(PAIRS):
                value(0, 0, q)

            def body(g, par, first, last):
                proj(g, par)
                if not first:
                    out_stage(g - 1, 0)
                score_stage(g, par)
                if not first:
                    for q in range(1, PAIRS):
                        out_stage(g - 1, q)
                else:
                    pe.wait_ge(w_lo_ready, 2)
                if not last:
                    for q in range(PAIRS - 1):
                        value(g + 1, 1 - par, q)
                turn(g)
                if not last:
                    value(g + 1, 1 - par, PAIRS - 1)
                mix(g, par)

            run(pe, body)
            for q in range(PAIRS):
                out_stage(GROUPS - 1, q)

        @block.scalar
        def _(act):
            for dst, src in ((emb_sb, emb_t), (w1e_sb, w1_e), (w2e_sb, w2_e), (b1_sb, w1_b), (b2_sb, w2_b),
                             (gb_sb, gcn_b)):
                act.dma_start(dst[:], src).then_inc(small_loaded, 16)
            act.dma_start(wob_sb[:], wo_b.to_broadcast([P, HID])).then_inc(small_loaded, 16)

            def split_x(g, slot):
                act.wait_ge(xt_loaded[slot], 16 * (half(g, slot) + 1))
                if not isinstance(g, int) or g > 1:
                    act.wait_ge(score_mm, g - 1)
                act.copy(xt_hi[:, slot], xt_sb[:, slot]).then_inc(xhi, 1)

            def value_hi(g, slot, q):
                act.wait_ge(value_mm, PAIRS * g + q + 1)
                act.copy(hg_hi[:, slot, q, :], VALUE_BANK[q][:, 0:HID]).then_inc(hghi, 1)

            def normalise(g, slot):
                act.wait_ge(nmr_ready, g + 1)
                for q in range(PAIRS):
                    a = act.activation(y_sb[:, slot, q, :], y_sb[:, slot, q, :], ACT.Identity,
                                       bias=nmr[:, q:q + 1], scale=rstd[:, q:q + 1])
                a.then_inc(y_ready, 1)

            act.wait_ge(xt_loaded[0], 16)
            act.copy(xt_hi[:, 0], xt_sb[:, 0]).then_inc(xhi, 1)
            act.wait_ge(gcn_loaded, 16)
            act.copy(gcn_hi[:, :, 0:HID], gcn_sb[:]).then_inc(w_hi_ready, 1)
            for d in range(C):
                act.wait_ge(m_mm, d + 1)
                act.copy(m_hi[:, d, :], bank[d][:, 0:HID]).then_inc(m_hi_ready, 1)
            act.wait_ge(ruk_mm, 1)
            act.copy(gcn_hi[:, :, HID:HW], bank[5][:, C:2 * C].rearrange("p (c o) -> p c o", o=1)
                     .to_broadcast([P, C, 2])).then_inc(u_hi_ready, 1)
            act.wait_ge(wo_loaded, 16)
            act.copy(wo_hi[:], wo_sb[:]).then_inc(w_hi_ready, 1)
            for q in range(PAIRS):
                value_hi(0, 0, q)

            def body(g, par, first, last):
                for f in range(C):
                    act.wait_ge(proj_mm, C * g + f + 1)
                    act.activation(g_hi[:, f, :], PROJ_BANK[f][:, 0:GT], ACT.Identity,
                                   bias=r_sb[:, f:f + 1]).then_inc(ghi, 1)
                if not last:
                    split_x(g + 1, 1 - par)
                act.wait_ge(masked, 3 * (g + 1))
                for q in range(PAIRS):
                    a = act.activation(prob[:, q, :], rel[:, q, :], ACT.Exp, bias=nmax[:, q:q + 1],
                                       accum_out=psum_row[:, q:q + 1])
                a.then_inc(expd, 1)
                if not last:
                    for q in range(2):
                        value_hi(g + 1, 1 - par, q)
                if not first:
                    normalise(g - 1, 1 - par)
                if not last:
                    value_hi(g + 1, 1 - par, 2)
                act.wait_ge(turn_mm, g + 1)
                act.copy(at_hi[:], score[:, 0:GT]).then_inc(athi, 1)
                if not last:
                    value_hi(g + 1, 1 - par, 3)
                for f in range(C):
                    act.wait_ge(mix_mm, C * g + f + 1)
                    act.activation(hs_sb[:, f, :], MIX_BANK[f][:, 0:GT], ACT.Relu,
                                   bias=gb_sb[:, f:f + 1]).then_inc(hsr, 1)

            run(act, body)
            normalise(GROUPS - 1, 1)

        @block.vector
        def _(dve):
            def value_lo(g, slot, q):
                dve.wait_ge(hghi, PAIRS * g + q + 1)
                dve.tensor_scalar(srow[:, slot, q:q + 1], VALUE_BANK[q][:, HID:HID + 1], k_sb[:, 0:1], None,
                                  ALU.add)
                dve.tensor_tensor(hg_lo[:, slot, q, :], VALUE_BANK[q][:, 0:HID], f32(hg_hi[:, slot, q, :]),
                                  ALU.subtract).then_inc(hglo, 1)

            def residual(g, slot, q):
                if q == 0:
                    dve.wait_ge(xb, g + 1)
                    if not isinstance(g, int) or g > 1:
                        dve.wait_ge(stored[slot], 16 * half(g, slot))
                dve.wait_ge(out_mm, PAIRS * g + q + 1)
                dve.tensor_tensor(y_sb[:, slot, q, :], OUT_BANK[q][:, 0:HID], x_sb[:, slot, q, :],
                                  ALU.add).then_inc(added, 1)
                dve.wait_ge(added, PAIRS * g + q + 1)
                dve.bn_stats(stats[:, q, :], y_sb[:, slot, q, :]).then_inc(statd, 1)

            def moments(g):
                for q in range(PAIRS):
                    dve.bn_aggr(mv[:, q, :], stats[:, q, :]).then_inc(aggrd, 1)

            def shift(g):
                dve.wait_ge(rstd_ready, g + 1)
                dve.scalar_tensor_tensor(nmr[:], mv[:, :, 0], -1.0, rstd[:], ALU.mult, ALU.mult).then_inc(nmr_ready, 1)

            dve.memset(attn[:], 0.0).then_inc(attn_zero, 1)
            dve.wait_ge(c_mm, 1)
            dve.wait_ge(small_loaded, 16 * 7)
            dve.tensor_tensor(c1_sb[:], bank[4][:, 0:C], b1_sb[:], ALU.add).then_inc(c_ready, 1)
            dve.tensor_tensor(c2_sb[:], bank[4][:, C:2 * C], b2_sb[:], ALU.add).then_inc(c_ready, 1)
            dve.wait_ge(w_hi_ready, 1)
            dve.tensor_tensor(gcn_lo[:, :, 0:HID], gcn_sb[:], f32(gcn_hi[:, :, 0:HID]), ALU.subtract)
            for d in range(C):
                dve.wait_ge(m_hi_ready, d + 1)
                dve.tensor_tensor(m_lo[:, d, :], bank[d][:, 0:HID], f32(m_hi[:, d, :]),
                                  ALU.subtract).then_inc(m_lo_ready, 1)
            dve.wait_ge(u_hi_ready, 1)
            dve.tensor_copy(r_sb[:], bank[5][:, 0:C])
            dve.tensor_copy(k_sb[:], bank[5][:, 2 * C:2 * C + 1])
            dve.tensor_tensor(gcn_lo[:, :, HID:HW], bank[5][:, C:2 * C].rearrange("p (c o) -> p c o", o=1)
                              .to_broadcast([P, C, 2]), f32(gcn_hi[:, :, HID:HW]),
                              ALU.subtract).then_inc(ruk_ready, 1)
            dve.wait_ge(ruk_ready, 1)
            dve.tensor_copy(nmax[:], r_sb[:, 0:1].to_broadcast([P, PAIRS])).then_inc(w_lo_ready, 1)
            dve.wait_ge(w_hi_ready, 2)
            dve.tensor_tensor(wo_lo[:], wo_sb[:], f32(wo_hi[:]), ALU.subtract).then_inc(w_lo_ready, 1)
            for q in range(PAIRS):
                value_lo(0, 0, q)

            def body(g, par, first, last):
                for f in range(C):
                    dve.wait_ge(ghi, C * g + f + 1)
                    dve.scalar_tensor_tensor(g_lo[:, f, :], PROJ_BANK[f][:, 0:GT], r_sb[:, f:f + 1],
                                             f32(g_hi[:, f, :]), ALU.add, ALU.subtract).then_inc(glo, 1)
                if not first:
                    residual(g - 1, 1 - par, 0)
                dve.wait_ge(score_mm, g + 1)
                dve.wait_ge(negm, g + 1)
                dve.wait_ge(hglo, PAIRS * (g + 1))
                if not first:
                    dve.wait_ge(expd, g)
                for q in range(PAIRS):
                    for h in range(2):
                        ps = slice(h * NODES, (h + 1) * NODES)
                        a = dve.scalar_tensor_tensor(
                            rel[ps, q, :], score[ps, q * P + h * NODES:q * P + (h + 1) * NODES],
                            srow[ps, par, q:q + 1], adj_sb[ps, par, q, :], ALU.add, ALU.mult)
                a.then_inc(masked, 1)
                dve.wait_ge(masked, 3 * g + 1)
                dve.tensor_tensor(rel[:], rel[:], neg_sb[:, par], ALU.add).then_inc(masked, 1)
                dve.wait_ge(masked, 3 * g + 2)
                dve.tensor_reduce(nmax[:], rel[:], AX_X, ALU.max, negate=True).then_inc(masked, 1)
                if not first:
                    residual(g - 1, 1 - par, 1)
                    residual(g - 1, 1 - par, 2)
                dve.wait_ge(expd, g + 1)
                dve.reciprocal(rsum[:], psum_row[:]).then_inc(normed, 1)
                dve.wait_ge(normed, 2 * g + 1)
                if first:
                    dve.wait_ge(attn_zero, 1)
                for h in range(2):
                    ps = slice(h * NODES, (h + 1) * NODES)
                    a = dve.tensor_tensor(attn[ps, :, h * NODES:(h + 1) * NODES], prob[ps],
                                          rsum[ps, :].rearrange("p (q o) -> p q o", o=1)
                                          .to_broadcast([NODES, PAIRS, NODES]), ALU.mult)
                a.then_inc(normed, 1)
                if not first:
                    residual(g - 1, 1 - par, 3)
                    dve.wait_ge(statd, PAIRS * g)
                if not last:
                    value_lo(g + 1, 1 - par, 0)
                if not first:
                    moments(g - 1)
                    shift(g - 1)
                if not last:
                    value_lo(g + 1, 1 - par, 1)
                    value_lo(g + 1, 1 - par, 2)
                dve.wait_ge(athi, g + 1)
                dve.tensor_tensor(at_lo[:], score[:, 0:GT], f32(at_hi[:]), ALU.subtract).then_inc(atlo, 1)
                if not last:
                    value_lo(g + 1, 1 - par, 3)
                for f in range(C):
                    dve.wait_ge(hsr, C * g + f + 1)
                    dve.tensor_copy(hs_hi[:, f, :], hs_sb[:, f, :]).then_inc(hshi, 1)

            run(dve, body)
            for q in range(PAIRS):
                residual(GROUPS - 1, 1, q)
            dve.wait_ge(statd, PAIRS * GROUPS)
            moments(GROUPS - 1)
            shift(GROUPS - 1)

        @block.gpsimd
        def _(pool):
            def split_x(g, slot):
                pool.wait_ge(xhi, g + 1)
                pool.wait_ge(adj_loaded[slot], 16 * (half(g, slot) + 1))
                if not isinstance(g, int) or g > 1:
                    pool.wait_ge(masked, 3 * (g - 1))
                pool.tensor_tensor(xt_lo[:, slot], xt_sb[:, slot], f32(xt_hi[:, slot]),
                                   ALU.subtract).then_inc(xlo, 1)

            def mask(g, slot):
                pool.tensor_scalar(neg_sb[:, slot], adj_sb[:, slot], NEG, -NEG, ALU.mult, ALU.add).then_inc(negm, 1)

            def bias_x(g, slot):
                pool.wait_ge(x_loaded[slot], 16 * (half(g, slot) + 1))
                pool.tensor_tensor(x_sb[:, slot], x_sb[:, slot],
                                   wob_sb[:].rearrange("p (o n) -> p o n", o=1).to_broadcast([P, PAIRS, HID]),
                                   ALU.add).then_inc(xb, 1)

            def inverse_std(g):
                pool.wait_ge(aggrd, PAIRS * (g + 1))
                pool.tensor_tensor(veps[:], mv[:, :, 1], eps_sb[:], ALU.add).then_inc(veps_ready, 1)
                pool.wait_ge(veps_ready, g + 1)
                pool.tensor_tensor(rstd[:], veps[:], mhalf[:], ALU.pow).then_inc(rstd_ready, 1)

            pool.memset(mhalf[:], -0.5)
            pool.memset(eps_sb[:], EPS)
            pool.memset(ident[:], 0.0).then_inc(ident_zero, 1)
            pool.wait_ge(ident_zero, 1)
            pool.affine_select(out=ident[:], in_=ident[:], compare_op=ALU.not_equal, fill=1.0, base=0,
                               pattern=[[-1, P]], channel_multiplier=1).then_inc(ident_ready, 1)
            split_x(0, 0)
            mask(0, 0)
            pool.wait_ge(small_loaded, 16 * 7)
            bias_x(0, 0)

            def body(g, par, first, last):
                if not last:
                    split_x(g + 1, 1 - par)
                    mask(g + 1, 1 - par)
                if not first:
                    inverse_std(g - 1)
                if not last:
                    bias_x(g + 1, 1 - par)
                for f in range(C):
                    pool.wait_ge(hshi, C * g + f + 1)
                    pool.tensor_tensor(hs_lo[:, f, :], hs_sb[:, f, :], f32(hs_hi[:, f, :]),
                                       ALU.subtract).then_inc(hslo, 1)

            run(pool, body)
            inverse_std(GROUPS - 1)


def kernel(x, adj, L0_gnn_dep_emb_table, L0_gnn_W1_w, L0_gnn_W1_b, L0_gnn_W2_w, L0_gnn_W2_b,
           L0_gnn_gcn_w, L0_gnn_gcn_b, L0_gnn_Wo_w, L0_gnn_Wo_b):
    import numpy as np
    import concourse.bacc as bacc
    from concourse.bass_utils import run_bass_kernel_spmd

    x = np.asarray(x)
    hid = x.shape[2]
    w1, w2 = np.asarray(L0_gnn_W1_w), np.asarray(L0_gnn_W2_w)

    def columns(b):
        return np.asarray(b).reshape(-1, P).T

    laid_out = {
        "x": x,
        "x_t": x.reshape(-1, hid).T,
        "adj": np.asarray(adj),
        "emb_t": np.asarray(L0_gnn_dep_emb_table).T,
        "w1_t": w1[:hid].T,
        "w1_e": w1[hid:],
        "w1_b": columns(L0_gnn_W1_b),
        "w2_t": w2[:hid].T,
        "w2_e": w2[hid:],
        "w2_b": columns(L0_gnn_W2_b),
        "gcn_w": np.asarray(L0_gnn_gcn_w),
        "gcn_b": columns(L0_gnn_gcn_b),
        "wo_w": np.asarray(L0_gnn_Wo_w),
        "wo_b": np.asarray(L0_gnn_Wo_b).reshape(1, hid),
    }
    nc = bacc.Bacc("TRN2", target_bir_lowering=False, num_devices=1)
    arrays, args = {}, []
    for name, a in laid_out.items():
        a = np.ascontiguousarray(a)
        arrays[f"in_{name}_dram"] = a
        args.append(nc.dram_tensor(f"in_{name}_dram", a.shape, mybir.dt.from_np(a.dtype), kind="ExternalInput").ap())
    out = nc.dram_tensor("out_0_dram", x.shape, F32, kind="ExternalOutput").ap()
    gnn_layernorm_kernel(nc, *args, out)
    result = run_bass_kernel_spmd(nc, [arrays], core_ids=[0])
    return result.results[0]["out_0_dram"]
```

```python
from contextlib import ExitStack

import concourse.bass as bass
from concourse import mybir

F32 = mybir.dt.float32
F32R = mybir.dt.float32r
I32 = mybir.dt.int32
ALU = mybir.AluOpType
ACT = mybir.ActivationFunctionType
AX_X = mybir.AxisListType.X

P = 128
NEG = 1.0e9
EPS = 1e-5


def gnn_layernorm_kernel(nc, x, x_t, adj, edge, biases, w1_t, w2_t, gcn_w, wo_w, wo_b, out):
    HID, TOKENS = x_t.shape
    NODES = adj.shape[2]
    EDIM, NTYPES = edge.shape[0], edge.shape[1] - 2 * HID
    C = HID // P
    PAIRS = 4
    GT = PAIRS * P
    GROUPS = TOKENS // GT
    HALVES = PAIRS // 2
    HW = HID + 2
    assert 2 * NODES == P and GROUPS % 2 == 0 and GROUPS >= 4

    x_rows = x.rearrange("b n d -> (b n) d").rearrange("(g q p) d -> g p q d", q=PAIRS, p=P)
    out_rows = out.rearrange("b n d -> (b n) d").rearrange("(g q p) d -> g p q d", q=PAIRS, p=P)
    xt_cols = x_t.rearrange("(c p) (g t) -> g p c t", p=P, t=GT)
    adj_rows = adj.rearrange("b i j -> (b i) j").rearrange("(g q p) j -> g p q j", q=PAIRS, p=P)

    with ExitStack() as ctx:
        def sb(name, shape, dt=F32):
            return ctx.enter_context(nc.sbuf_tensor(name, shape, dt))

        def sem(name):
            return ctx.enter_context(nc.semaphore(name))

        ident = sb("ident", [P, P])
        w1t_sb = sb("w1t_sb", [P, C, HID])
        w2t_sb = sb("w2t_sb", [P, C, HID + 1])
        edge_sb = sb("edge_sb", [EDIM, NTYPES + 2 * HID])
        emb_sb = edge_sb[:, 0:NTYPES]
        w1e_sb = edge_sb[:, NTYPES:NTYPES + HID]
        w2e_sb = edge_sb[:, NTYPES + HID:NTYPES + 2 * HID]
        bias_sb = sb("bias_sb", [P, 3 * C])
        b1_sb, b2_sb, gb_sb = (bias_sb[:, n * C:(n + 1) * C] for n in range(3))
        wob_sb = sb("wob_sb", [P, HID])
        gcn_sb = sb("gcn_sb", [P, C, HID])
        wo_sb = sb("wo_sb", [P, C, HID])
        c1_sb = sb("c1_sb", [P, C])
        r_sb = sb("r_sb", [P, C])
        k_sb = sb("k_sb", [P, 1])
        m_hi = sb("m_hi", [P, C, HID], F32R)
        m_lo = sb("m_lo", [P, C, HID], F32R)
        gcn_hi = sb("gcn_hi", [P, C, HW], F32R)
        gcn_lo = sb("gcn_lo", [P, C, HW], F32R)
        wo_hi = sb("wo_hi", [P, C, HID], F32R)
        wo_lo = sb("wo_lo", [P, C, HID], F32R)
        xt_sb = sb("xt_sb", [P, 2, C, GT])
        xt_hi = sb("xt_hi", [P, 2, C, GT], F32R)
        xt_lo = sb("xt_lo", [P, 2, C, GT], F32R)
        x_sb = sb("x_sb", [P, 2, PAIRS, HID])
        adj_sb = sb("adj_sb", [P, 2, PAIRS, NODES], I32)
        neg_sb = sb("neg_sb", [P, 2, PAIRS, NODES])
        gt_sb = sb("gt_sb", [P, C, GT])
        hg_sb = sb("hg_sb", [P, 2, PAIRS, HID + 1])
        srow = sb("srow", [P, PAIRS])
        rel = sb("rel", [P, PAIRS, NODES])
        nmax = sb("nmax", [P, PAIRS])
        prob = sb("prob", [P, PAIRS, NODES])
        psum_row = sb("psum_row", [P, PAIRS])
        rsum = sb("rsum", [P, PAIRS])
        attn = sb("attn", [P, PAIRS, P])
        at_sb = sb("at_sb", [P, GT])
        hs_sb = sb("hs_sb", [P, C, GT])
        hs_hi = sb("hs_hi", [P, C, GT], F32R)
        hs_lo = sb("hs_lo", [P, C, GT], F32R)
        y_sb = sb("y_sb", [P, 2, PAIRS, HID])
        stats = sb("stats", [P, PAIRS, 6])
        mv = sb("mv", [P, PAIRS, 2])
        veps = sb("veps", [P, PAIRS])
        mhalf = sb("mhalf", [P, PAIRS])
        eps_sb = sb("eps_sb", [P, PAIRS])
        rstd = sb("rstd", [P, PAIRS])
        nmr = sb("nmr", [P, PAIRS])

        bank = [ctx.enter_context(nc.psum_tensor(f"bank{i}", [P, 512], F32)) for i in range(8)]
        PROJ_BANK = bank[0:3]
        OUT_BANK = bank[3:7]
        VALUE_BANK = bank[0:4]
        MIX_BANK = bank[4:7]
        score = bank[7]

        edge_loaded = sem("edge_loaded")
        bias_loaded = sem("bias_loaded")
        w1_loaded = sem("w1_loaded")
        w2_loaded = sem("w2_loaded")
        gcn_loaded = sem("gcn_loaded")
        wob_loaded = sem("wob_loaded")
        wo_loaded = sem("wo_loaded")
        xt_loaded = [sem(f"xt_loaded{i}") for i in range(2)]
        x_loaded = [sem(f"x_loaded{i}") for i in range(2)]
        adj_loaded = [sem(f"adj_loaded{i}") for i in range(2)]
        stored = [sem(f"stored{i}") for i in range(2)]
        ident_zero = sem("ident_zero")
        ident_ready = sem("ident_ready")
        attn_zero = sem("attn_zero")
        c_mm = sem("c_mm")
        c_ready = sem("c_ready")
        m_mm = sem("m_mm")
        m_hi_ready = sem("m_hi_ready")
        m_lo_ready = sem("m_lo_ready")
        rk_mm = sem("rk_mm")
        rk_ready = sem("rk_ready")
        gcn_hi_ready = sem("gcn_hi_ready")
        gcn_lo_ready = sem("gcn_lo_ready")
        wo_hi_ready = sem("wo_hi_ready")
        wo_lo_ready = sem("wo_lo_ready")
        xhi = sem("xhi")
        xlo = sem("xlo")
        negm = sem("negm")
        xb = sem("xb")
        proj_mm = sem("proj_mm")
        gt_ready = sem("gt_ready")
        score_mm = sem("score_mm")
        value_mm = sem("value_mm")
        hg_ready = sem("hg_ready")
        srow_ready = sem("srow_ready")
        masked = sem("masked")
        expd = sem("expd")
        normed = sem("normed")
        turn_mm = sem("turn_mm")
        at_ready = sem("at_ready")
        mix_mm = sem("mix_mm")
        hsr = sem("hsr")
        hshi = sem("hshi")
        hslo = sem("hslo")
        out_mm = sem("out_mm")
        added = sem("added")
        statd = sem("statd")
        aggrd = sem("aggrd")
        veps_ready = sem("veps_ready")
        rstd_ready = sem("rstd_ready")
        nmr_ready = sem("nmr_ready")
        y_ready = sem("y_ready")

        def f32(ap):
            return ap.bitcast(F32)

        def run(eng, body):
            body(0, 0, True, False)
            with eng.Fori(0, (GROUPS - 2) // 2) as i:
                body(2 * i + 1, 1, False, False)
                body(2 * i + 2, 0, False, False)
            body(GROUPS - 1, 1, False, True)

        def half(g, slot):
            return g // 2 if isinstance(g, int) else (g - slot) // 2

        block = ctx.enter_context(nc.Block())

        @block.sync
        def _(sp):
            sp.dma_start(edge_sb[:], edge).then_inc(edge_loaded, 16)
            sp.dma_start(w2t_sb[:, :, 0:HID], w2_t.rearrange("(c p) n -> p c n", p=P)).then_inc(w2_loaded, 16)
            sp.dma_start(w1t_sb[:], w1_t.rearrange("(c p) n -> p c n", p=P)).then_inc(w1_loaded, 16)
            sp.dma_start(gcn_sb[:], gcn_w.rearrange("(c p) n -> p c n", p=P)).then_inc(gcn_loaded, 16)
            sp.dma_start(adj_sb[:, 0], adj_rows[0]).then_inc(adj_loaded[0], 16)
            sp.dma_start(xt_sb[:, 1], xt_cols[1]).then_inc(xt_loaded[1], 16)
            sp.dma_start(wob_sb[:], wo_b.to_broadcast([P, HID])).then_inc(wob_loaded, 16)
            sp.dma_start(wo_sb[:], wo_w.rearrange("(c p) n -> p c n", p=P)).then_inc(wo_loaded, 16)
            sp.dma_start(adj_sb[:, 1], adj_rows[1]).then_inc(adj_loaded[1], 16)
            sp.dma_start(x_sb[:, 0], x_rows[0]).then_inc(x_loaded[0], 16)

            def store(g, slot, h):
                qs = slice(2 * h, 2 * h + 2)
                sp.wait_ge(y_ready, HALVES * g + h + 1)
                sp.dma_start(out_rows[g][:, qs], y_sb[:, slot, qs]).then_inc(stored[slot], 16)

            sp.dma_start(x_sb[:, 1], x_rows[1]).then_inc(x_loaded[1], 16)
            with sp.Fori(0, (GROUPS - 2) // 2) as i:
                for par in (1, 0):
                    g = 2 * i + 2 - par
                    sp.wait_ge(score_mm, g)
                    sp.wait_ge(xlo, g)
                    sp.dma_start(xt_sb[:, 1 - par], xt_cols[g + 1]).then_inc(xt_loaded[1 - par], 16)
                    sp.wait_ge(masked, 3 * g)
                    sp.dma_start(adj_sb[:, 1 - par], adj_rows[g + 1]).then_inc(adj_loaded[1 - par], 16)
                    sp.wait_ge(added, PAIRS * g)
                    sp.dma_start(x_sb[:, 1 - par], x_rows[g + 1]).then_inc(x_loaded[1 - par], 16)
                    for h in range(HALVES):
                        store(g - 1, 1 - par, h)
            for g in (GROUPS - 2, GROUPS - 1):
                for h in range(HALVES):
                    store(g, g % 2, h)
            for slot in range(2):
                sp.wait_ge(stored[slot], 16 * HALVES * (GROUPS // 2))

        @block.tensor
        def _(pe):
            def three(acc, a_hi, a_lo, b_hi, b_lo, first, last):
                pe.matmul(acc, a_hi, b_hi, start=first, stop=False)
                pe.matmul(acc, a_hi, b_lo, start=False, stop=False)
                return pe.matmul(acc, a_lo, b_hi, start=False, stop=last)

            def proj(g, par):
                pe.wait_ge(xlo, g + 1)
                for f in range(C):
                    pe.wait_ge(hg_ready, PAIRS * g + f + 1)
                    fs = slice(f * P, (f + 1) * P)
                    for c in range(C):
                        mm = three(PROJ_BANK[f][:, 0:GT], m_hi[:, c, fs], m_lo[:, c, fs],
                                   xt_hi[:, par, c, :], xt_lo[:, par, c, :], c == 0, c == C - 1)
                    mm.then_inc(proj_mm, 1)

            def score_stage(g, par):
                pe.wait_ge(gt_ready, C * (g + 1))
                if not (isinstance(g, int) and g == 0):
                    pe.wait_ge(at_ready, g)
                for q in range(PAIRS):
                    ts = slice(q * P, (q + 1) * P)
                    for c in range(C):
                        mm = pe.matmul(score[:, ts], gt_sb[:, c, ts], xt_sb[:, par, c, ts],
                                       start=(c == 0), stop=(c == C - 1))
                mm.then_inc(score_mm, 1)

            def value(g, par, q):
                pe.wait_ge(xlo, g + 1)
                if not isinstance(g, int) or g > 0:
                    if q < C:
                        pe.wait_ge(gt_ready, C * (g - 1) + q + 1)
                    elif not isinstance(g, int) or g > 1:
                        pe.wait_ge(added, PAIRS * (g - 2) + 1)
                ts = slice(q * P, (q + 1) * P)
                for c in range(C):
                    mm = three(VALUE_BANK[q][:, 0:HW], xt_hi[:, par, c, ts], xt_lo[:, par, c, ts],
                               gcn_hi[:, c, :], gcn_lo[:, c, :], c == 0, c == C - 1)
                mm.then_inc(value_mm, 1)

            def turn(g):
                pe.wait_ge(normed, 2 * (g + 1))
                for q in range(PAIRS):
                    mm = pe.transpose(score[:, q * P:(q + 1) * P], attn[:, q, :], ident[:])
                mm.then_inc(turn_mm, 1)

            def mix(g, par):
                pe.wait_ge(at_ready, g + 1)
                for f in range(C):
                    if not (isinstance(g, int) and g == 0):
                        pe.wait_ge(added, PAIRS * (g - 1) + f + 2)
                    for q in range(PAIRS):
                        ts = slice(q * P, (q + 1) * P)
                        mm = pe.matmul(MIX_BANK[f][:, ts], hg_sb[:, par, q, f * P:(f + 1) * P], at_sb[:, ts],
                                       start=True, stop=True)
                    mm.then_inc(mix_mm, 1)

            def out_stage(g, q):
                pe.wait_ge(hslo, C * (g + 1))
                if q == 0:
                    if not isinstance(g, int) or g < GROUPS - 1:
                        pe.wait_ge(hg_ready, PAIRS * (g + 2))
                else:
                    pe.wait_ge(hsr, C * g + q)
                ts = slice(q * P, (q + 1) * P)
                for c in range(C):
                    mm = three(OUT_BANK[q][:, 0:HID], hs_hi[:, c, ts], hs_lo[:, c, ts],
                               wo_hi[:, c, :], wo_lo[:, c, :], c == 0, c == C - 1)
                mm.then_inc(out_mm, 1)

            pe.wait_ge(edge_loaded, 16)
            for n, w in enumerate((w1e_sb, w2e_sb)):
                for c in range(C):
                    mm = pe.matmul(bank[4][:, n * C + c:n * C + c + 1], w[:, c * P:(c + 1) * P], emb_sb[:, 1:2],
                                   start=True, stop=True)
            mm.then_inc(c_mm, 1)
            pe.wait_ge(w2_loaded, 16)
            pe.wait_ge(w1_loaded, 16)
            pe.wait_ge(c_ready, 2)
            for d in range(C):
                for c in range(C):
                    mm = pe.matmul(bank[d][:, 0:HID + 1], w1t_sb[:, c, d * P:(d + 1) * P], w2t_sb[:, c, :],
                                   start=(c == 0), stop=(c == C - 1))
                mm.then_inc(m_mm, 1)
            for d in range(C):
                for c in range(C):
                    pe.matmul(bank[5][:, d:d + 1], w2t_sb[:, c, d * P:(d + 1) * P], c1_sb[:, c:c + 1],
                              start=(c == 0), stop=(c == C - 1))
            for c in range(C):
                mm = pe.matmul(bank[5][:, C:C + 1], c1_sb[:, c:c + 1].to_broadcast([P, P]),
                               w2t_sb[:, c, HID:HID + 1], start=(c == 0), stop=(c == C - 1))
            mm.then_inc(rk_mm, 1)

            pe.wait_ge(gcn_lo_ready, 1)
            pe.wait_ge(m_lo_ready, C)
            for q in range(PAIRS):
                value(0, 0, q)

            def body(g, par, first, last):
                proj(g, par)
                if not first:
                    out_stage(g - 1, 0)
                score_stage(g, par)
                if first:
                    pe.wait_ge(wo_lo_ready, 1)
                    pe.wait_ge(ident_ready, 1)
                else:
                    for q in range(1, PAIRS):
                        out_stage(g - 1, q)
                if not last:
                    for q in range(PAIRS - 1):
                        value(g + 1, 1 - par, q)
                turn(g)
                if not last:
                    value(g + 1, 1 - par, PAIRS - 1)
                mix(g, par)

            run(pe, body)
            for q in range(PAIRS):
                out_stage(GROUPS - 1, q)

        @block.scalar
        def _(act):
            act.dma_start(bias_sb[:], biases).then_inc(bias_loaded, 16)
            act.dma_start(xt_sb[:, 0], xt_cols[0]).then_inc(xt_loaded[0], 16)

            def split_x(g, slot):
                act.wait_ge(xt_loaded[slot], 16 * (half(g, slot) + 1))
                act.copy(xt_hi[:, slot], xt_sb[:, slot]).then_inc(xhi, 1)

            def normalise(g, slot, h):
                act.wait_ge(nmr_ready, HALVES * g + h + 1)
                for q in (2 * h, 2 * h + 1):
                    a = act.activation(y_sb[:, slot, q, :], y_sb[:, slot, q, :], ACT.Identity,
                                       bias=nmr[:, q:q + 1], scale=rstd[:, q:q + 1])
                a.then_inc(y_ready, 1)

            split_x(0, 0)
            act.wait_ge(gcn_loaded, 16)
            act.copy(gcn_hi[:, :, 0:HID], gcn_sb[:]).then_inc(gcn_hi_ready, 1)
            for d in range(C):
                act.wait_ge(m_mm, d + 1)
                act.copy(gcn_hi[:, d, HID:HW], bank[d][:, HID:HID + 1].to_broadcast([P, 2]))
                act.copy(m_hi[:, d, :], bank[d][:, 0:HID]).then_inc(m_hi_ready, 1)
            act.wait_ge(wo_loaded, 16)
            act.copy(wo_hi[:], wo_sb[:]).then_inc(wo_hi_ready, 1)
            act.wait_ge(rk_ready, 1)
            act.wait_ge(bias_loaded, 16)

            def body(g, par, first, last):
                for f in range(C):
                    act.wait_ge(proj_mm, C * g + f + 1)
                    act.activation(gt_sb[:, f, :], PROJ_BANK[f][:, 0:GT], ACT.Identity,
                                   bias=r_sb[:, f:f + 1]).then_inc(gt_ready, 1)
                if not last:
                    split_x(g + 1, 1 - par)
                act.wait_ge(masked, 3 * (g + 1))
                for q in range(PAIRS):
                    a = act.activation(prob[:, q, :], rel[:, q, :], ACT.Exp, bias=nmax[:, q:q + 1],
                                       accum_out=psum_row[:, q:q + 1])
                a.then_inc(expd, 1)
                if not first:
                    normalise(g - 1, 1 - par, 0)
                act.wait_ge(turn_mm, g + 1)
                act.copy(at_sb[:], score[:, 0:GT]).then_inc(at_ready, 1)
                if not first:
                    normalise(g - 1, 1 - par, 1)
                for f in range(C):
                    act.wait_ge(mix_mm, C * g + f + 1)
                    act.activation(hs_sb[:, f, :], MIX_BANK[f][:, 0:GT], ACT.Relu,
                                   bias=gb_sb[:, f:f + 1]).then_inc(hsr, 1)

            run(act, body)
            for h in range(HALVES):
                normalise(GROUPS - 1, 1, h)

        @block.vector
        def _(dve):
            def value_out(g, slot, q):
                dve.wait_ge(value_mm, PAIRS * g + q + 1)
                dve.tensor_copy(hg_sb[:, slot, q, :], VALUE_BANK[q][:, 0:HID + 1]).then_inc(hg_ready, 1)

            def residual(g, slot, q):
                if q == 0:
                    dve.wait_ge(xb, g + 1)
                    if not isinstance(g, int) or g > 1:
                        dve.wait_ge(stored[slot], 16 * HALVES * half(g, slot))
                dve.wait_ge(out_mm, PAIRS * g + q + 1)
                dve.tensor_tensor(y_sb[:, slot, q, :], OUT_BANK[q][:, 0:HID], x_sb[:, slot, q, :],
                                  ALU.add).then_inc(added, 1)
                dve.wait_ge(added, PAIRS * g + q + 1)
                dve.bn_stats(stats[:, q, :], y_sb[:, slot, q, :]).then_inc(statd, 1)

            def moments(h):
                for q in (2 * h, 2 * h + 1):
                    a = dve.bn_aggr(mv[:, q, :], stats[:, q, :])
                a.then_inc(aggrd, 1)

            def shift(g, h):
                qs = slice(2 * h, 2 * h + 2)
                dve.wait_ge(rstd_ready, HALVES * g + h + 1)
                dve.scalar_tensor_tensor(nmr[:, qs], mv[:, qs, 0], -1.0, rstd[:, qs],
                                         ALU.mult, ALU.mult).then_inc(nmr_ready, 1)

            dve.memset(attn[:], 0.0).then_inc(attn_zero, 1)
            dve.wait_ge(c_mm, 1)
            dve.wait_ge(bias_loaded, 16)
            dve.tensor_tensor(w2t_sb[:, :, HID], bank[4][:, C:2 * C], b2_sb, ALU.add).then_inc(c_ready, 1)
            dve.tensor_tensor(c1_sb[:], bank[4][:, 0:C], b1_sb, ALU.add).then_inc(c_ready, 1)
            dve.wait_ge(gcn_hi_ready, 1)
            dve.tensor_tensor(gcn_lo[:, :, 0:HID], gcn_sb[:], f32(gcn_hi[:, :, 0:HID]),
                              ALU.subtract).then_inc(gcn_lo_ready, 1)
            for d in range(C):
                dve.wait_ge(m_hi_ready, d + 1)
                dve.tensor_tensor(gcn_lo[:, d, HID:HW], bank[d][:, HID:HID + 1].to_broadcast([P, 2]),
                                  f32(gcn_hi[:, d, HID:HW]), ALU.subtract)
                dve.tensor_tensor(m_lo[:, d, :], bank[d][:, 0:HID], f32(m_hi[:, d, :]),
                                  ALU.subtract).then_inc(m_lo_ready, 1)
            dve.wait_ge(rk_mm, 1)
            dve.tensor_copy(k_sb[:], bank[5][:, C:C + 1])
            dve.tensor_copy(r_sb[:], bank[5][:, 0:C]).then_inc(rk_ready, 1)
            for q in range(PAIRS):
                value_out(0, 0, q)
            dve.wait_ge(wo_hi_ready, 1)
            dve.tensor_tensor(wo_lo[:], wo_sb[:], f32(wo_hi[:]), ALU.subtract).then_inc(wo_lo_ready, 1)

            def body(g, par, first, last):
                dve.wait_ge(hg_ready, PAIRS * (g + 1))
                dve.tensor_scalar(srow[:], hg_sb[:, par, :, HID], k_sb[:, 0:1], None, ALU.add).then_inc(srow_ready, 1)
                if not first:
                    residual(g - 1, 1 - par, 0)
                dve.wait_ge(score_mm, g + 1)
                dve.wait_ge(negm, g + 1)
                dve.wait_ge(srow_ready, g + 1)
                if not first:
                    dve.wait_ge(expd, g)
                for q in range(PAIRS):
                    for h in range(2):
                        ps = slice(h * NODES, (h + 1) * NODES)
                        a = dve.scalar_tensor_tensor(
                            rel[ps, q, :], score[ps, q * P + h * NODES:q * P + (h + 1) * NODES],
                            srow[ps, q:q + 1], adj_sb[ps, par, q, :], ALU.add, ALU.mult)
                a.then_inc(masked, 1)
                dve.wait_ge(masked, 3 * g + 1)
                dve.tensor_tensor(rel[:], rel[:], neg_sb[:, par], ALU.add).then_inc(masked, 1)
                dve.wait_ge(masked, 3 * g + 2)
                dve.tensor_reduce(nmax[:], rel[:], AX_X, ALU.max, negate=True).then_inc(masked, 1)
                if not first:
                    residual(g - 1, 1 - par, 1)
                    dve.wait_ge(statd, PAIRS * (g - 1) + 2)
                dve.wait_ge(expd, g + 1)
                dve.reciprocal(rsum[:], psum_row[:]).then_inc(normed, 1)
                dve.wait_ge(normed, 2 * g + 1)
                if first:
                    dve.wait_ge(attn_zero, 1)
                for h in range(2):
                    ps = slice(h * NODES, (h + 1) * NODES)
                    a = dve.tensor_tensor(attn[ps, :, h * NODES:(h + 1) * NODES], prob[ps],
                                          rsum[ps, :].rearrange("p (q o) -> p q o", o=1)
                                          .to_broadcast([NODES, PAIRS, NODES]), ALU.mult)
                a.then_inc(normed, 1)
                if not first:
                    moments(0)
                    residual(g - 1, 1 - par, 2)
                    shift(g - 1, 0)
                    residual(g - 1, 1 - par, 3)
                    dve.wait_ge(statd, PAIRS * g)
                if not last:
                    value_out(g + 1, 1 - par, 0)
                if not first:
                    moments(1)
                if not last:
                    value_out(g + 1, 1 - par, 1)
                if not first:
                    shift(g - 1, 1)
                if not last:
                    value_out(g + 1, 1 - par, 2)
                    value_out(g + 1, 1 - par, 3)
                for f in range(C):
                    dve.wait_ge(hsr, C * g + f + 1)
                    dve.tensor_copy(hs_hi[:, f, :], hs_sb[:, f, :]).then_inc(hshi, 1)

            run(dve, body)
            g = GROUPS - 1
            for h in range(HALVES):
                residual(g, 1, 2 * h)
                residual(g, 1, 2 * h + 1)
                dve.wait_ge(statd, PAIRS * g + 2 * h + 2)
                moments(h)
                shift(g, h)

        @block.gpsimd
        def _(pool):
            def split_x(g, slot):
                pool.wait_ge(xhi, g + 1)
                pool.wait_ge(adj_loaded[slot], 16 * (half(g, slot) + 1))
                if not isinstance(g, int) or g > 1:
                    pool.wait_ge(masked, 3 * (g - 1))
                pool.tensor_tensor(xt_lo[:, slot], xt_sb[:, slot], f32(xt_hi[:, slot]),
                                   ALU.subtract).then_inc(xlo, 1)

            def mask(g, slot):
                pool.tensor_scalar(neg_sb[:, slot], adj_sb[:, slot], NEG, -NEG, ALU.mult, ALU.add).then_inc(negm, 1)

            def bias_x(g, slot):
                pool.wait_ge(x_loaded[slot], 16 * (half(g, slot) + 1))
                pool.tensor_tensor(x_sb[:, slot], x_sb[:, slot],
                                   wob_sb[:].rearrange("p (o n) -> p o n", o=1).to_broadcast([P, PAIRS, HID]),
                                   ALU.add).then_inc(xb, 1)

            def inverse_std(g, h):
                qs = slice(2 * h, 2 * h + 2)
                n = HALVES * g + h + 1
                pool.wait_ge(aggrd, n)
                pool.tensor_tensor(veps[:, qs], mv[:, qs, 1], eps_sb[:, qs], ALU.add).then_inc(veps_ready, 1)
                pool.wait_ge(veps_ready, n)
                pool.tensor_tensor(rstd[:, qs], veps[:, qs], mhalf[:, qs], ALU.pow).then_inc(rstd_ready, 1)

            pool.memset(mhalf[:], -0.5)
            pool.memset(eps_sb[:], EPS)
            pool.memset(ident[:], 0.0).then_inc(ident_zero, 1)
            pool.wait_ge(ident_zero, 1)
            pool.affine_select(out=ident[:], in_=ident[:], compare_op=ALU.not_equal, fill=1.0, base=0,
                               pattern=[[-1, P]], channel_multiplier=1).then_inc(ident_ready, 1)
            split_x(0, 0)
            mask(0, 0)
            pool.wait_ge(wob_loaded, 16)
            bias_x(0, 0)

            def body(g, par, first, last):
                if not last:
                    split_x(g + 1, 1 - par)
                    mask(g + 1, 1 - par)
                if not first:
                    inverse_std(g - 1, 0)
                    inverse_std(g - 1, 1)
                if not last:
                    bias_x(g + 1, 1 - par)
                for f in range(C):
                    pool.wait_ge(hshi, C * g + f + 1)
                    pool.tensor_tensor(hs_lo[:, f, :], hs_sb[:, f, :], f32(hs_hi[:, f, :]),
                                       ALU.subtract).then_inc(hslo, 1)

            run(pool, body)
            for h in range(HALVES):
                inverse_std(GROUPS - 1, h)


def kernel(x, adj, L0_gnn_dep_emb_table, L0_gnn_W1_w, L0_gnn_W1_b, L0_gnn_W2_w, L0_gnn_W2_b,
           L0_gnn_gcn_w, L0_gnn_gcn_b, L0_gnn_Wo_w, L0_gnn_Wo_b):
    import numpy as np
    import concourse.bacc as bacc
    from concourse.bass_utils import run_bass_kernel_spmd

    x = np.asarray(x)
    hid = x.shape[2]
    w1, w2 = np.asarray(L0_gnn_W1_w), np.asarray(L0_gnn_W2_w)

    def columns(b):
        return np.asarray(b).reshape(-1, P).T

    laid_out = {
        "x": x,
        "x_t": x.reshape(-1, hid).T,
        "adj": np.asarray(adj),
        "edge": np.concatenate([np.asarray(L0_gnn_dep_emb_table).T, w1[hid:], w2[hid:]], axis=1),
        "biases": np.concatenate([columns(b) for b in (L0_gnn_W1_b, L0_gnn_W2_b, L0_gnn_gcn_b)], axis=1),
        "w1_t": w1[:hid].T,
        "w2_t": w2[:hid].T,
        "gcn_w": np.asarray(L0_gnn_gcn_w),
        "wo_w": np.asarray(L0_gnn_Wo_w),
        "wo_b": np.asarray(L0_gnn_Wo_b).reshape(1, hid),
    }
    nc = bacc.Bacc("TRN2", target_bir_lowering=False, num_devices=1)
    arrays, args = {}, []
    for name, a in laid_out.items():
        a = np.ascontiguousarray(a)
        arrays[f"in_{name}_dram"] = a
        args.append(nc.dram_tensor(f"in_{name}_dram", a.shape, mybir.dt.from_np(a.dtype), kind="ExternalInput").ap())
    out = nc.dram_tensor("out_0_dram", x.shape, F32, kind="ExternalOutput").ap()
    gnn_layernorm_kernel(nc, *args, out)
    result = run_bass_kernel_spmd(nc, [arrays], core_ids=[0])
    return result.results[0]["out_0_dram"]
```

```python
from contextlib import ExitStack

import concourse.bass as bass
from concourse import mybir

F32 = mybir.dt.float32
F32R = mybir.dt.float32r
I32 = mybir.dt.int32
ALU = mybir.AluOpType
ACT = mybir.ActivationFunctionType
AX_X = mybir.AxisListType.X
AX_XY = mybir.AxisListType.XY

P = 128
NEG = 1.0e9
EPS = 1e-5
WARM_UP = 3


def gnn_layernorm_kernel(nc, x, x_t, adj, adj_t, edge, biases, w1_t, w2_t, gcn_w, wo_w, wo_b, out):
    HID, TOKENS = x_t.shape
    NODES = adj.shape[2]
    EDIM, NTYPES = edge.shape[0], edge.shape[1] - 2 * HID
    C = HID // P
    PAIRS = 4
    GT = PAIRS * P
    GROUPS = TOKENS // GT
    HALVES = PAIRS // 2
    HW = HID + 2
    assert 2 * NODES == P and GROUPS % 2 == 0 and GROUPS >= 4

    x_rows = x.rearrange("b n d -> (b n) d").rearrange("(g q p) d -> g p q d", q=PAIRS, p=P)
    out_rows = out.rearrange("b n d -> (b n) d").rearrange("(g q p) d -> g p q d", q=PAIRS, p=P)
    xt_cols = x_t.rearrange("(c p) (g t) -> g p c t", p=P, t=GT)
    adj_rows = adj.rearrange("b i j -> (b i) j").rearrange("(g q p) j -> g p q j", q=PAIRS, p=P)

    x_pair = x.rearrange("b n d -> (b n) d").rearrange("(m p) d -> m p d", p=P)
    out_pair = out.rearrange("b n d -> (b n) d").rearrange("(m p) d -> m p d", p=P)
    xt_pair = x_t.rearrange("(c p) (m t) -> m p c t", p=P, t=P)
    adj_pair = adj.rearrange("b i j -> (b i) j").rearrange("(m p) j -> m p j", p=P)
    adjt_pair = adj_t.rearrange("b j i -> (b j) i").rearrange("(m p) i -> m p i", p=P)

    with ExitStack() as ctx:
        def sb(name, shape, dt=F32):
            return ctx.enter_context(nc.sbuf_tensor(name, shape, dt))

        def sem(name):
            return ctx.enter_context(nc.semaphore(name))

        ident = sb("ident", [P, P])
        w1t_sb = sb("w1t_sb", [P, C, HID])
        w2t_sb = sb("w2t_sb", [P, C, HID + 1])
        edge_sb = sb("edge_sb", [EDIM, NTYPES + 2 * HID])
        emb_sb = edge_sb[:, 0:NTYPES]
        w1e_sb = edge_sb[:, NTYPES:NTYPES + HID]
        w2e_sb = edge_sb[:, NTYPES + HID:NTYPES + 2 * HID]
        bias_sb = sb("bias_sb", [P, 3 * C])
        b1_sb, b2_sb, gb_sb = (bias_sb[:, n * C:(n + 1) * C] for n in range(3))
        wob_sb = sb("wob_sb", [P, HID])
        gcn_sb = sb("gcn_sb", [P, C, HID])
        wo_sb = sb("wo_sb", [P, C, HID])
        c1_sb = sb("c1_sb", [P, C])
        c2_sb = sb("c2_sb", [P, C])
        r_sb = sb("r_sb", [P, C])
        k_sb = sb("k_sb", [P, 1])
        m_hi = sb("m_hi", [P, C, HID], F32R)
        m_lo = sb("m_lo", [P, C, HID], F32R)
        gcn_hi = sb("gcn_hi", [P, C, HW], F32R)
        gcn_lo = sb("gcn_lo", [P, C, HW], F32R)
        wo_hi = sb("wo_hi", [P, C, HID], F32R)
        wo_lo = sb("wo_lo", [P, C, HID], F32R)
        xt_sb = sb("xt_sb", [P, 2, C, GT])
        xt_hi = sb("xt_hi", [P, 2, C, GT], F32R)
        xt_lo = sb("xt_lo", [P, 2, C, GT], F32R)
        x_sb = sb("x_sb", [P, 2, PAIRS, HID])
        adj_sb = sb("adj_sb", [P, 2, PAIRS, NODES], I32)
        neg_sb = sb("neg_sb", [P, 2, PAIRS, NODES])
        gt_sb = sb("gt_sb", [P, C, GT])
        hg_sb = sb("hg_sb", [P, 2, PAIRS, HID + 1])
        srow = sb("srow", [P, PAIRS])
        rel = sb("rel", [P, PAIRS, NODES])
        nmax = sb("nmax", [P, PAIRS])
        prob = sb("prob", [P, PAIRS, NODES])
        psum_row = sb("psum_row", [P, PAIRS])
        rsum = sb("rsum", [P, PAIRS])
        attn = sb("attn", [P, PAIRS, P])
        at_sb = sb("at_sb", [P, GT])
        hs_sb = sb("hs_sb", [P, C, GT])
        hs_hi = sb("hs_hi", [P, C, GT], F32R)
        hs_lo = sb("hs_lo", [P, C, GT], F32R)
        y_sb = sb("y_sb", [P, 2, PAIRS, HID])
        stats = sb("stats", [P, PAIRS, 6])
        mv = sb("mv", [P, PAIRS, 2])
        veps = sb("veps", [P, PAIRS])
        mhalf = sb("mhalf", [P, PAIRS])
        eps_sb = sb("eps_sb", [P, PAIRS])
        rstd = sb("rstd", [P, PAIRS])
        nmr = sb("nmr", [P, PAIRS])

        adj_max = sb("adj_max", [P, PAIRS, NODES], I32)
        row_max = sb("row_max", [P, 1])
        all_max = sb("all_max", [1, 1])
        general = sb("general", [1, 1], I32)
        kinds = sb("kinds", [P, NTYPES], I32)
        ones = sb("ones", [P, 1])
        c1_all = sb("c1_all", [P, C, NTYPES])
        c2_all = sb("c2_all", [P, C, NTYPES])
        c12_all = sb("c12_all", [P, C, NTYPES])
        u_all = sb("u_all", [P, C, NTYPES])
        r_all = sb("r_all", [P, C, NTYPES])
        k_all = sb("k_all", [P, NTYPES])
        xu_sb = sb("xu_sb", [P, NTYPES])
        xr_sb = sb("xr_sb", [P, NTYPES])
        onehot = sb("onehot", [P, NODES, NTYPES])
        pick_u = sb("pick_u", [P, NODES])
        pick_r = sb("pick_r", [P, P])
        edges = sb("edges", [P, NODES])

        bank = [ctx.enter_context(nc.psum_tensor(f"bank{i}", [P, 512], F32)) for i in range(8)]
        PROJ_BANK = bank[0:3]
        VALUE_BANK = [bank[0], bank[1], bank[3], bank[2]]
        OUT_BANK = bank[3:7]
        MIX_BANK = bank[4:7]
        score = bank[7]
        M_BANK = bank[4:7]
        C_BANK = bank[2], bank[7]

        edge_loaded = sem("edge_loaded")
        bias_loaded = sem("bias_loaded")
        w12_loaded = [sem(f"w12_loaded{c}") for c in range(C)]
        gcn_loaded = sem("gcn_loaded")
        wob_loaded = sem("wob_loaded")
        wo_loaded = sem("wo_loaded")
        xt0_loaded = sem("xt0_loaded")
        xt_loaded = [sem(f"xt_loaded{i}") for i in range(2)]
        x_loaded = [sem(f"x_loaded{i}") for i in range(2)]
        adj_loaded = [sem(f"adj_loaded{i}") for i in range(2)]
        stored = [sem(f"stored{i}") for i in range(2)]
        max_zero = sem("max_zero")
        adjmax = sem("adjmax")
        rowmax_ready = sem("rowmax_ready")
        rowmax_mm = sem("rowmax_mm")
        allmax_ready = sem("allmax_ready")
        general_ready = sem("general_ready")
        ident_zero = sem("ident_zero")
        ident_ready = sem("ident_ready")
        attn_zero = sem("attn_zero")
        c2_zero = sem("c2_zero")
        c2_mm = sem("c2_mm")
        c1_mm = sem("c1_mm")
        c2_ready = sem("c2_ready")
        c1_ready = sem("c1_ready")
        xt0_hi = sem("xt0_hi")
        xt0_lo = sem("xt0_lo")
        m_mm = sem("m_mm")
        m_hi_ready = sem("m_hi_ready")
        m_lo_ready = sem("m_lo_ready")
        rk_mm = sem("rk_mm")
        rk_ready = sem("rk_ready")
        gcn_hi_ready = sem("gcn_hi_ready")
        gcn_lo_ready = sem("gcn_lo_ready")
        wo_hi_ready = sem("wo_hi_ready")
        wo_lo_ready = sem("wo_lo_ready")
        xhi = sem("xhi")
        xlo = sem("xlo")
        negm = sem("negm")
        xb = sem("xb")
        proj_mm = sem("proj_mm")
        gt_ready = sem("gt_ready")
        score_mm = sem("score_mm")
        value_mm = sem("value_mm")
        hg_ready = sem("hg_ready")
        srow_ready = sem("srow_ready")
        masked = sem("masked")
        expd = sem("expd")
        normed = sem("normed")
        turn_mm = sem("turn_mm")
        at_ready = sem("at_ready")
        mix_mm = sem("mix_mm")
        hsr = sem("hsr")
        hshi = sem("hshi")
        hslo = sem("hslo")
        hslo1 = sem("hslo1")
        out_mm = sem("out_mm")
        added = sem("added")
        statd = sem("statd")
        aggrd = sem("aggrd")
        veps_ready = sem("veps_ready")
        rstd_ready = sem("rstd_ready")
        y_ready = sem("y_ready")
        nmr_ready = sem("nmr_ready")
        y_end = sem("y_end")

        kinds_ready = sem("kinds_ready")
        zero_ready = sem("zero_ready")
        c_all_mm = sem("c_all_mm")
        c_all_ready = sem("c_all_ready")
        c12_ready = sem("c12_ready")
        tables_mm = sem("tables_mm")
        tables_ready = sem("tables_ready")
        pair_xt_loaded = sem("pair_xt_loaded")
        pair_x_loaded = sem("pair_x_loaded")
        pair_adj_loaded = sem("pair_adj_loaded")
        pair_x_mm = sem("pair_x_mm")
        pair_x_ready = sem("pair_x_ready")
        pair_pick = sem("pair_pick")
        pair_score_mm = sem("pair_score_mm")
        pair_rel = sem("pair_rel")
        pair_exp = sem("pair_exp")
        pair_rsum = sem("pair_rsum")
        pair_attn = sem("pair_attn")
        pair_turn_mm = sem("pair_turn_mm")
        pair_at_ready = sem("pair_at_ready")
        pair_mix_mm = sem("pair_mix_mm")
        pair_hs_ready = sem("pair_hs_ready")
        pair_out_mm = sem("pair_out_mm")
        pair_y = sem("pair_y")
        pair_aggr = sem("pair_aggr")
        pair_veps = sem("pair_veps")
        pair_rstd = sem("pair_rstd")
        pair_y_ready = sem("pair_y_ready")
        pair_stored = sem("pair_stored")

        def is_general(eng):
            eng.wait_ge(general_ready, 1)
            return eng.value_load(general[0:1, 0:1], min_val=0, max_val=1) > 0

        def f32(ap):
            return ap.bitcast(F32)

        def run(eng, body):
            body(0, 0, True, False)
            with eng.Fori(0, (GROUPS - 2) // 2) as i:
                body(2 * i + 1, 1, False, False)
                body(2 * i + 2, 0, False, False)
            body(GROUPS - 1, 1, False, True)

        def half(g, slot):
            return g // 2 if isinstance(g, int) else (g - slot) // 2

        STORES = [HALVES * (GROUPS // 2), HALVES * (GROUPS // 2 - 1) + PAIRS]

        block = ctx.enter_context(nc.Block())

        @block.sync
        def _(sp):
            for slot in range(2):
                sp.sem_inc(stored[slot], 1)
            sp.dma_start(edge_sb[:], edge).then_inc(edge_loaded, 16)
            for c in range(C):
                sp.dma_start(w2t_sb[:, c, 0:HID], w2_t[c * P:(c + 1) * P]).then_inc(w12_loaded[c], 16)
                sp.dma_start(w1t_sb[:, c], w1_t[c * P:(c + 1) * P]).then_inc(w12_loaded[c], 16)
            sp.dma_start(xt_sb[:, 0, :, 0:GT // 2], xt_cols[0][:, :, 0:GT // 2]).then_inc(xt0_loaded, 16)
            sp.dma_start(gcn_sb[:], gcn_w.rearrange("(c p) n -> p c n", p=P)).then_inc(gcn_loaded, 16)
            sp.dma_start(xt_sb[:, 0, :, GT // 2:GT], xt_cols[0][:, :, GT // 2:GT]).then_inc(xt_loaded[0], 16)
            sp.dma_start(adj_sb[:, 0], adj_rows[0]).then_inc(adj_loaded[0], 16)
            sp.dma_start(xt_sb[:, 1], xt_cols[1]).then_inc(xt_loaded[1], 16)
            sp.dma_start(wob_sb[:], wo_b.to_broadcast([P, HID])).then_inc(wob_loaded, 16)
            sp.dma_start(wo_sb[:], wo_w.rearrange("(c p) n -> p c n", p=P)).then_inc(wo_loaded, 16)
            sp.dma_start(adj_sb[:, 1], adj_rows[1]).then_inc(adj_loaded[1], 16)
            sp.dma_start(x_sb[:, 0], x_rows[0]).then_inc(x_loaded[0], 16)

            def store(g, slot, h):
                qs = slice(2 * h, 2 * h + 2)
                sp.wait_ge(y_ready, HALVES * g + h + 1)
                sp.dma_start(out_rows[g][:, qs], y_sb[:, slot, qs]).then_inc(stored[slot], 16)

            sp.dma_start(x_sb[:, 1], x_rows[1]).then_inc(x_loaded[1], 16)
            with sp.Fori(0, (GROUPS - 2) // 2) as i:
                for par in (1, 0):
                    g = 2 * i + 2 - par
                    sp.wait_ge(score_mm, g)
                    sp.wait_ge(xlo, g)
                    sp.dma_start(xt_sb[:, 1 - par], xt_cols[g + 1]).then_inc(xt_loaded[1 - par], 16)
                    sp.wait_ge(masked, 3 * g)
                    sp.wait_ge(adjmax, g)
                    sp.dma_start(adj_sb[:, 1 - par], adj_rows[g + 1]).then_inc(adj_loaded[1 - par], 16)
                    sp.wait_ge(added, PAIRS * g)
                    sp.dma_start(x_sb[:, 1 - par], x_rows[g + 1]).then_inc(x_loaded[1 - par], 16)
                    for h in range(HALVES):
                        store(g - 1, 1 - par, h)
            for h in range(HALVES):
                sp.wait_ge(y_end, h + 1)
                qs = slice(2 * h, 2 * h + 2)
                sp.dma_start(out_rows[GROUPS - 2][:, qs], y_sb[:, 0, qs]).then_inc(stored[0], 16)
            for q in range(PAIRS):
                if q < 2:
                    sp.wait_ge(y_end, HALVES + q + 1)
                else:
                    sp.wait_ge(y_ready, HALVES * (GROUPS - 2) + q - 1)
                sp.dma_start(out_rows[GROUPS - 1][:, q], y_sb[:, 1, q]).then_inc(stored[1], 16)
            again = is_general(sp)
            for slot in range(2):
                sp.wait_ge(stored[slot], 1 + 16 * STORES[slot])

            with sp.If(again):
                sp.sem_inc(pair_stored, 1)
                with sp.Fori(0, TOKENS // P) as n:
                    sp.wait_ge(pair_stored, 1 + 16 * n)
                    sp.dma_start(xt_sb[:, 0, :, 0:P], xt_pair[n]).then_inc(pair_xt_loaded, 16)
                    sp.dma_start(x_sb[:, 0, 0, :], x_pair[n]).then_inc(pair_x_loaded, 16)
                    sp.dma_start(adj_sb[:, 0, 0, :], adj_pair[n]).then_inc(pair_adj_loaded, 16)
                    sp.dma_start(adj_sb[:, 1, 0, :], adjt_pair[n]).then_inc(pair_adj_loaded, 16)
                    sp.wait_ge(pair_y_ready, n + 1)
                    sp.dma_start(out_pair[n], y_sb[:, 0, 0, :]).then_inc(pair_stored, 16)
                sp.wait_ge(pair_stored, 1 + 16 * (TOKENS // P))

        @block.tensor
        def _(pe):
            def three(acc, a_hi, a_lo, b_hi, b_lo, first, last):
                pe.matmul(acc, a_hi, b_hi, start=first, stop=False)
                pe.matmul(acc, a_hi, b_lo, start=False, stop=False)
                return pe.matmul(acc, a_lo, b_hi, start=False, stop=last)

            def proj(g, par):
                pe.wait_ge(xlo, g + 1)
                for f in range(C):
                    pe.wait_ge(hg_ready, PAIRS if isinstance(g, int) and g == 1 else PAIRS * g + min(f + 1, 2))
                    fs = slice(f * P, (f + 1) * P)
                    for c in range(C):
                        mm = three(PROJ_BANK[f][:, 0:GT], m_hi[:, c, fs], m_lo[:, c, fs],
                                   xt_hi[:, par, c, :], xt_lo[:, par, c, :], c == 0, c == C - 1)
                    mm.then_inc(proj_mm, 1)

            def score_stage(g, par):
                pe.wait_ge(gt_ready, C * (g + 1))
                if not (isinstance(g, int) and g == 0):
                    pe.wait_ge(at_ready, g)
                for q in range(PAIRS):
                    for c in range(C):
                        for h in range(2):
                            ts = slice(q * P + h * NODES, q * P + (h + 1) * NODES)
                            mm = pe.matmul(score[h * NODES:(h + 1) * NODES, ts], gt_sb[:, c, ts],
                                           xt_sb[:, par, c, ts], start=(c == 0), stop=(c == C - 1))
                mm.then_inc(score_mm, 1)

            def value(g, par, q):
                if isinstance(g, int) and g == 0 and q < 2:
                    pe.wait_ge(xt0_lo, 1)
                else:
                    pe.wait_ge(xlo, g + 1)
                if q < 2:
                    if isinstance(g, int) and g == 1:
                        pe.wait_ge(gt_ready, C + q + 1)
                    elif not isinstance(g, int) or g > 0:
                        pe.wait_ge(gt_ready, C * (g - 1) + q + 1)
                elif q == 2 and isinstance(g, int) and g == 1:
                    pe.wait_ge(hg_ready, 3)
                elif q == 3:
                    pe.wait_ge(gt_ready, C * (g + 1))
                ts = slice(q * P, (q + 1) * P)
                for c in range(C):
                    mm = three(VALUE_BANK[q][:, 0:HW], xt_hi[:, par, c, ts], xt_lo[:, par, c, ts],
                               gcn_hi[:, c, :], gcn_lo[:, c, :], c == 0, c == C - 1)
                mm.then_inc(value_mm, 1)

            def turn(g):
                pe.wait_ge(normed, 2 * (g + 1))
                for q in range(PAIRS):
                    mm = pe.transpose(score[:, q * P:(q + 1) * P], attn[:, q, :], ident[:])
                mm.then_inc(turn_mm, 1)

            def mix(g, par):
                pe.wait_ge(at_ready, g + 1)
                pe.wait_ge(hg_ready, PAIRS * (g + 1))
                for f in range(C):
                    if not (isinstance(g, int) and g == 0):
                        pe.wait_ge(added, PAIRS * (g - 1) + f + 2)
                    for q in range(PAIRS):
                        ts = slice(q * P, (q + 1) * P)
                        mm = pe.matmul(MIX_BANK[f][:, ts], hg_sb[:, par, q, f * P:(f + 1) * P], at_sb[:, ts],
                                       start=True, stop=True)
                    mm.then_inc(mix_mm, 1)

            def out_chunk(g, q, c):
                if c == 0:
                    if q > 0:
                        pe.wait_ge(hsr, C * g + q)
                    elif not (isinstance(g, int) and g == GROUPS - 1):
                        pe.wait_ge(hg_ready, PAIRS * (g + 1) + 3)
                ts = slice(q * P, (q + 1) * P)
                acc = OUT_BANK[q][:, 0:HID]
                pe.wait_ge(hshi, C * g + c + 1)
                pe.matmul(acc, hs_hi[:, c, ts], wo_hi[:, c, :], start=(c == 0), stop=False)
                pe.matmul(acc, hs_hi[:, c, ts], wo_lo[:, c, :], start=False, stop=False)
                if c == 1:
                    pe.wait_ge(hslo1, g + 1)
                else:
                    pe.wait_ge(hslo, 2 * g + (1 if c == 0 else 2))
                mm = pe.matmul(acc, hs_lo[:, c, ts], wo_hi[:, c, :], start=False, stop=(c == C - 1))
                if c == C - 1:
                    mm.then_inc(out_mm, 1)

            def c_stage(n, w, done):
                for c in range(C):
                    mm = pe.matmul(C_BANK[n][:, c:c + 1], w[:, c * P:(c + 1) * P], emb_sb[:, 1:2],
                                   start=True, stop=True)
                mm.then_inc(done, 1)

            pe.wait_ge(attn_zero, 1)
            for _ in range(WARM_UP):
                pe.matmul(OUT_BANK[0][:, 0:HID], attn[:, 0, :], attn[:, 0:C, :].rearrange("p q n -> p (q n)"),
                          start=True, stop=True)
            pe.wait_ge(c2_zero, 1)
            for c in range(C):
                pe.wait_ge(w12_loaded[c], 32)
                for d in range(C):
                    mm = pe.matmul(M_BANK[d][:, 0:HID + 1], w1t_sb[:, c, d * P:(d + 1) * P], w2t_sb[:, c, :],
                                   start=(c == 0), stop=(c == C - 1))
                    if c == 0 and d == 0:
                        pe.wait_ge(edge_loaded, 16)
                        c_stage(1, w2e_sb, c2_mm)
                    if c == C - 1:
                        mm.then_inc(m_mm, 1)
                if c == 0:
                    pe.wait_ge(c2_ready, 1)
                    for d in range(C):
                        pe.matmul(M_BANK[d][:, HID:HID + 1], w1t_sb[:, 0, d * P:(d + 1) * P],
                                  c2_sb[:, 0:1], start=False, stop=False)
            c_stage(0, w1e_sb, c1_mm)

            pe.wait_ge(gcn_lo_ready, 1 + C)
            value(0, 0, 0)
            pe.wait_ge(c1_ready, 1)
            for d in range(C):
                for c in range(C):
                    pe.matmul(score[:, d:d + 1], w2t_sb[:, c, d * P:(d + 1) * P], c1_sb[:, c:c + 1],
                              start=(c == 0), stop=(c == C - 1))
            value(0, 0, 1)
            for c in range(C):
                mm = pe.matmul(score[:, C:C + 1], c1_sb[:, c:c + 1].to_broadcast([P, P]),
                               c2_sb[:, c:c + 1], start=(c == 0), stop=(c == C - 1))
            mm.then_inc(rk_mm, 1)
            pe.wait_ge(m_lo_ready, C)
            proj(0, 0)
            value(0, 0, 2)
            value(0, 0, 3)

            def body(g, par, first, last):
                score_stage(g, par)
                if first:
                    proj(1, 1)
                    pe.wait_ge(ident_ready, 1)
                    pe.wait_ge(wo_lo_ready, 1)
                else:
                    for q in range(PAIRS):
                        for c in range(C):
                            out_chunk(g - 1, q, c)
                    if not last:
                        value(g + 1, 1 - par, 0)
                turn(g)
                if first:
                    value(1, 1, 0)
                elif not last:
                    value(g + 1, 1 - par, 1)
                mix(g, par)
                if first:
                    value(1, 1, 1)
                elif not last:
                    proj(g + 1, 1 - par)
                if not last:
                    value(g + 1, 1 - par, 2)
                    value(g + 1, 1 - par, 3)

            run(pe, body)
            for c in range(C):
                for q in range(PAIRS - 1):
                    out_chunk(GROUPS - 1, q, c)
            for c in range(C):
                out_chunk(GROUPS - 1, PAIRS - 1, c)

            pe.wait_ge(rowmax_ready, 1)
            pe.wait_ge(at_ready, GROUPS)
            pe.transpose(score[0:1, 0:P], row_max[:], ident[:]).then_inc(rowmax_mm, 1)

            with pe.If(is_general(pe)):
                for slot in range(2):
                    pe.wait_ge(stored[slot], 1 + 16 * STORES[slot])
                for n, w in enumerate((w1e_sb, w2e_sb)):
                    for c in range(C):
                        mm = pe.matmul(bank[n][:, c * NTYPES:(c + 1) * NTYPES], w[:, c * P:(c + 1) * P], emb_sb,
                                       start=True, stop=True)
                mm.then_inc(c_all_mm, 1)
                pe.wait_ge(c_all_ready, 1)
                pe.wait_ge(c12_ready, 1)
                for n, (w, c_all) in enumerate(((w1t_sb, c2_all), (w2t_sb, c1_all))):
                    for f in range(C):
                        for c in range(C):
                            pe.matmul(bank[2 + n][:, f * NTYPES:(f + 1) * NTYPES], w[:, c, f * P:(f + 1) * P],
                                      c_all[:, c, :], start=(c == 0), stop=(c == C - 1))
                for c in range(C):
                    mm = pe.matmul(bank[4][:, 0:NTYPES], ones[:].to_broadcast([P, P]), c12_all[:, c, :],
                                   start=(c == 0), stop=(c == C - 1))
                mm.then_inc(tables_mm, 1)
                pe.wait_ge(tables_ready, 1)

                with pe.Fori(0, TOKENS // P) as n:
                    pe.wait_ge(pair_xt_loaded, 16 * (n + 1))
                    for f in range(C):
                        for c in range(C):
                            for part in (m_hi, m_lo):
                                pe.matmul(bank[0][:, f * P:(f + 1) * P], f32(part[:, c, f * P:(f + 1) * P]),
                                          xt_sb[:, 0, c, 0:P], start=(c == 0 and part is m_hi),
                                          stop=(c == C - 1 and part is m_lo))
                    for acc, table in ((bank[1][:, 0:HID], gcn_sb), (bank[2][:, 0:NTYPES], u_all),
                                       (bank[3][:, 0:NTYPES], r_all)):
                        for c in range(C):
                            mm = pe.matmul(acc, xt_sb[:, 0, c, 0:P], table[:, c, :],
                                           start=(c == 0), stop=(c == C - 1))
                    mm.then_inc(pair_x_mm, 1)
                    pe.wait_ge(pair_x_ready, n + 1)
                    for c in range(C):
                        pe.matmul(score[:, 0:P], gt_sb[:, c, 0:P], xt_sb[:, 0, c, 0:P], start=(c == 0), stop=False)
                    pe.wait_ge(pair_pick, 6 * n + 3)
                    pe.matmul(score[:, 0:P], pick_r[:], ident[:], start=False, stop=True).then_inc(pair_score_mm, 1)
                    pe.wait_ge(pair_attn, n + 1)
                    pe.transpose(score[:, P:2 * P], attn[:, 0, :], ident[:]).then_inc(pair_turn_mm, 1)
                    pe.wait_ge(pair_at_ready, n + 1)
                    for f in range(C):
                        mm = pe.matmul(bank[4][:, f * P:(f + 1) * P], hg_sb[:, 0, 0, f * P:(f + 1) * P],
                                       at_sb[:, 0:P], start=True, stop=True)
                    mm.then_inc(pair_mix_mm, 1)
                    pe.wait_ge(pair_hs_ready, n + 1)
                    for c in range(C):
                        mm = pe.matmul(bank[5][:, 0:HID], hs_sb[:, c, 0:P], wo_sb[:, c, :],
                                       start=(c == 0), stop=(c == C - 1))
                    mm.then_inc(pair_out_mm, 1)

        @block.scalar
        def _(act):
            act.dma_start(bias_sb[:], biases).then_inc(bias_loaded, 16)

            def split_x(g, slot):
                act.wait_ge(xt_loaded[slot], 16 * (half(g, slot) + 1))
                act.copy(xt_hi[:, slot], xt_sb[:, slot]).then_inc(xhi, 1)

            def project_out(g, chunks=range(C)):
                for f in chunks:
                    act.wait_ge(proj_mm, C * g + f + 1)
                    act.activation(gt_sb[:, f, :], PROJ_BANK[f][:, 0:GT], ACT.Identity,
                                   bias=r_sb[:, f:f + 1]).then_inc(gt_ready, 1)

            def normalise(g, slot, part, pairs):
                act.wait_ge(nmr_ready, part + 1)
                for q in pairs:
                    a = act.activation(y_sb[:, slot, q, :], y_sb[:, slot, q, :], ACT.Identity,
                                       bias=nmr[:, q:q + 1], scale=rstd[:, q:q + 1])
                a.then_inc(y_end, 1)

            act.wait_ge(xt0_loaded, 16)
            act.copy(xt_hi[:, 0, :, 0:GT // 2], xt_sb[:, 0, :, 0:GT // 2]).then_inc(xt0_hi, 1)
            act.wait_ge(gcn_loaded, 16)
            act.copy(gcn_hi[:, :, 0:HID], gcn_sb[:]).then_inc(gcn_hi_ready, 1)
            act.wait_ge(xt_loaded[0], 16)
            act.copy(xt_hi[:, 0, :, GT // 2:GT], xt_sb[:, 0, :, GT // 2:GT]).then_inc(xhi, 1)
            for d in range(C):
                act.wait_ge(m_mm, d + 1)
                act.copy(gcn_hi[:, d, HID:HW],
                         M_BANK[d][:, HID:HID + 1].to_broadcast([P, 2])).then_inc(gcn_hi_ready, 1)
            for d in range(C):
                act.wait_ge(gcn_lo_ready, d + 2)
                act.copy(m_hi[:, d, :], M_BANK[d][:, 0:HID]).then_inc(m_hi_ready, 1)
            split_x(1, 1)
            act.wait_ge(wo_loaded, 16)
            act.copy(wo_hi[:], wo_sb[:]).then_inc(wo_hi_ready, 1)
            act.wait_ge(rk_ready, 1)
            act.wait_ge(bias_loaded, 16)
            project_out(0)

            def body(g, par, first, last):
                if not first and not last:
                    split_x(g + 1, 1 - par)
                if first:
                    project_out(1, (0,))
                act.wait_ge(masked, 3 * (g + 1))
                for q in range(PAIRS):
                    a = act.activation(prob[:, q, :], rel[:, q, :], ACT.Exp, bias=nmax[:, q:q + 1],
                                       accum_out=psum_row[:, q:q + 1])
                a.then_inc(expd, 1)
                if first:
                    project_out(1, (1, 2))
                act.wait_ge(turn_mm, g + 1)
                act.copy(at_sb[:], score[:, 0:GT]).then_inc(at_ready, 1)
                for f in range(C):
                    act.wait_ge(mix_mm, C * g + f + 1)
                    act.activation(hs_sb[:, f, :], MIX_BANK[f][:, 0:GT], ACT.Relu,
                                   bias=gb_sb[:, f:f + 1]).then_inc(hsr, 1)
                if last:
                    normalise(g - 1, 0, 0, (0, 1))
                    normalise(g - 1, 0, 1, (2, 3))
                elif not first:
                    project_out(g + 1)

            run(act, body)
            for q in (0, 1):
                normalise(GROUPS - 1, 1, HALVES + q, (q,))

            with act.If(is_general(act)):
                with act.Fori(0, TOKENS // P) as n:
                    act.wait_ge(pair_rel, 5 * (n + 1))
                    act.activation(prob[:, 0, :], rel[:, 0, :], ACT.Exp, bias=nmax[:, 0:1],
                                   accum_out=psum_row[:, 0:1]).then_inc(pair_exp, 1)
                    act.wait_ge(pair_turn_mm, n + 1)
                    act.copy(at_sb[:, 0:P], score[:, P:2 * P]).then_inc(pair_at_ready, 1)
                    act.wait_ge(pair_mix_mm, n + 1)
                    for f in range(C):
                        a = act.activation(hs_sb[:, f, 0:P], bank[4][:, f * P:(f + 1) * P], ACT.Relu,
                                           bias=gb_sb[:, f:f + 1])
                    a.then_inc(pair_hs_ready, 1)

        @block.vector
        def _(dve):
            def value_out(g, slot, q):
                dve.wait_ge(value_mm, PAIRS * g + q + 1)
                dve.tensor_copy(hg_sb[:, slot, q, :], VALUE_BANK[q][:, 0:HID + 1]).then_inc(hg_ready, 1)

            def add_x(g, slot, q):
                if q == 0:
                    dve.wait_ge(xb, g + 1)
                    dve.wait_ge(stored[slot], 1 + 16 * HALVES * half(g, slot))
                dve.wait_ge(out_mm, PAIRS * g + q + 1)
                dve.tensor_tensor(y_sb[:, slot, q, :], OUT_BANK[q][:, 0:HID], x_sb[:, slot, q, :],
                                  ALU.add).then_inc(added, 1)

            def statistics(g, slot, q):
                dve.wait_ge(added, PAIRS * g + q + 1)
                dve.bn_stats(stats[:, q, :], y_sb[:, slot, q, :]).then_inc(statd, 1)

            def residual(g, slot, q):
                add_x(g, slot, q)
                statistics(g, slot, q)

            def moments(pairs):
                for q in pairs:
                    a = dve.bn_aggr(mv[:, q, :], stats[:, q, :])
                a.then_inc(aggrd, 1)

            def normalise(g, slot, n, pairs):
                dve.wait_ge(rstd_ready, HALVES * g + n)
                for q in pairs:
                    a = dve.tensor_scalar(y_sb[:, slot, q, :], y_sb[:, slot, q, :], mv[:, q, 0:1], rstd[:, q:q + 1],
                                          ALU.subtract, ALU.mult)
                a.then_inc(y_ready, 1)

            dve.memset(w2t_sb[:, 0, HID:HID + 1], 0.0).then_inc(c2_zero, 1)
            dve.memset(attn[:], 0.0).then_inc(attn_zero, 1)
            dve.memset(adj_max[:], 0).then_inc(max_zero, 1)
            dve.wait_ge(bias_loaded, 16)
            dve.wait_ge(c2_mm, 1)
            dve.tensor_tensor(c2_sb[:], C_BANK[1][:, 0:C], b2_sb, ALU.add)
            dve.tensor_tensor(w2t_sb[:, 1:C, HID], C_BANK[1][:, 1:C], b2_sb[:, 1:C], ALU.add).then_inc(c2_ready, 1)
            halves = [slice(0, GT // 2), slice(GT // 2, GT)]
            dve.wait_ge(xt0_hi, 1)
            dve.tensor_tensor(xt_lo[:, 0, :, halves[0]], xt_sb[:, 0, :, halves[0]], f32(xt_hi[:, 0, :, halves[0]]),
                              ALU.subtract).then_inc(xt0_lo, 1)
            dve.wait_ge(gcn_hi_ready, 1)
            dve.tensor_tensor(gcn_lo[:, :, 0:HID], gcn_sb[:], f32(gcn_hi[:, :, 0:HID]),
                              ALU.subtract).then_inc(gcn_lo_ready, 1)
            for d in range(C):
                dve.wait_ge(gcn_hi_ready, d + 2)
                dve.tensor_tensor(gcn_lo[:, d, HID:HW], M_BANK[d][:, HID:HID + 1].to_broadcast([P, 2]),
                                  f32(gcn_hi[:, d, HID:HW]), ALU.subtract).then_inc(gcn_lo_ready, 1)
            dve.wait_ge(c1_mm, 1)
            dve.tensor_tensor(c1_sb[:], C_BANK[0][:, 0:C], b1_sb, ALU.add).then_inc(c1_ready, 1)
            dve.wait_ge(xhi, 1)
            dve.tensor_tensor(xt_lo[:, 0, :, halves[1]], xt_sb[:, 0, :, halves[1]], f32(xt_hi[:, 0, :, halves[1]]),
                              ALU.subtract).then_inc(xlo, 1)
            for d in range(C):
                dve.wait_ge(m_hi_ready, d + 1)
                dve.tensor_tensor(m_lo[:, d, :], M_BANK[d][:, 0:HID], f32(m_hi[:, d, :]),
                                  ALU.subtract).then_inc(m_lo_ready, 1)
            value_out(0, 0, 0)
            dve.wait_ge(rk_mm, 1)
            dve.tensor_copy(k_sb[:], score[:, C:C + 1])
            dve.tensor_copy(r_sb[:], score[:, 0:C]).then_inc(rk_ready, 1)
            value_out(0, 0, 1)
            dve.wait_ge(wo_hi_ready, 1)
            dve.tensor_tensor(wo_lo[:], wo_sb[:], f32(wo_hi[:]), ALU.subtract).then_inc(wo_lo_ready, 1)
            for q in range(2, PAIRS):
                value_out(0, 0, q)

            def body(g, par, first, last):
                dve.wait_ge(hg_ready, PAIRS * (g + 1))
                dve.tensor_scalar(srow[:], hg_sb[:, par, :, HID], k_sb[:, 0:1], None, ALU.add).then_inc(srow_ready, 1)
                dve.wait_ge(score_mm, g + 1)
                dve.wait_ge(negm, g + 1)
                dve.wait_ge(srow_ready, g + 1)
                if not first:
                    dve.wait_ge(expd, g)
                for q in range(PAIRS):
                    for h in range(2):
                        ps = slice(h * NODES, (h + 1) * NODES)
                        a = dve.scalar_tensor_tensor(
                            rel[ps, q, :], score[ps, q * P + h * NODES:q * P + (h + 1) * NODES],
                            srow[ps, q:q + 1], adj_sb[ps, par, q, :], ALU.add, ALU.mult)
                a.then_inc(masked, 1)
                dve.wait_ge(masked, 3 * g + 1)
                dve.tensor_tensor(rel[:], rel[:], neg_sb[:, par], ALU.add).then_inc(masked, 1)
                dve.wait_ge(masked, 3 * g + 2)
                dve.tensor_reduce(nmax[:], rel[:], AX_X, ALU.max, negate=True).then_inc(masked, 1)
                if not first:
                    residual(g - 1, 1 - par, 0)
                if first:
                    dve.wait_ge(max_zero, 1)
                else:
                    dve.wait_ge(adjmax, g)
                dve.tensor_tensor(adj_max[:], adj_max[:], adj_sb[:, par], ALU.max).then_inc(adjmax, 1)
                dve.wait_ge(expd, g + 1)
                dve.reciprocal(rsum[:], psum_row[:]).then_inc(normed, 1)
                dve.wait_ge(normed, 2 * g + 1)
                if first:
                    dve.wait_ge(attn_zero, 1)
                for h in range(2):
                    ps = slice(h * NODES, (h + 1) * NODES)
                    a = dve.tensor_tensor(attn[ps, :, h * NODES:(h + 1) * NODES], prob[ps],
                                          rsum[ps, :].rearrange("p (q o) -> p q o", o=1)
                                          .to_broadcast([NODES, PAIRS, NODES]), ALU.mult)
                a.then_inc(normed, 1)
                if not first:
                    residual(g - 1, 1 - par, 1)
                    dve.wait_ge(statd, PAIRS * (g - 1) + 2)
                    residual(g - 1, 1 - par, 2)
                    moments((0, 1))
                    residual(g - 1, 1 - par, 3)
                    dve.wait_ge(statd, PAIRS * g)
                if first:
                    value_out(1, 1, 0)
                elif not last:
                    value_out(g + 1, 1 - par, 0)
                    moments((2, 3))
                    normalise(g - 1, 1 - par, 1, (0, 1))
                    value_out(g + 1, 1 - par, 1)
                    normalise(g - 1, 1 - par, 2, (2, 3))
                else:
                    moments((2, 3))
                for f in range(C):
                    dve.wait_ge(hsr, C * g + f + 1)
                    dve.tensor_copy(hs_hi[:, f, :], hs_sb[:, f, :]).then_inc(hshi, 1)
                    if (f != 1) if last else (f == 1):
                        dve.wait_ge(hshi, C * g + f + 1)
                        dve.tensor_tensor(hs_lo[:, f, :], hs_sb[:, f, :], f32(hs_hi[:, f, :]),
                                          ALU.subtract).then_inc(hslo if last else hslo1, 1)
                if first:
                    value_out(1, 1, 1)
                if not last:
                    value_out(g + 1, 1 - par, 2)
                    value_out(g + 1, 1 - par, 3)
                if last:
                    dve.wait_ge(adjmax, GROUPS)
                    dve.tensor_reduce(row_max[:], adj_max[:], AX_XY, ALU.max).then_inc(rowmax_ready, 1)

            run(dve, body)
            g = GROUPS - 1
            for q in range(PAIRS):
                add_x(g, 1, q)
                if 2 <= q:
                    dve.wait_ge(statd, PAIRS * g + q - 1)
                    moments((q - 2,))
                if 1 <= q:
                    statistics(g, 1, q - 1)
            statistics(g, 1, PAIRS - 1)
            dve.wait_ge(statd, PAIRS * GROUPS)
            moments((2, 3))
            dve.wait_ge(rowmax_mm, 1)
            dve.tensor_reduce(all_max[:], score[0:1, 0:P], AX_X, ALU.max).then_inc(allmax_ready, 1)
            dve.wait_ge(allmax_ready, 1)
            dve.tensor_scalar(general[:], all_max[:], 1.0, None, ALU.is_gt).then_inc(general_ready, 1)
            for q in (2, 3):
                normalise(g, 1, HALVES + 1, (q,))

            with dve.If(is_general(dve)):
                dve.memset(ones[:], 1.0)
                dve.memset(pick_r[:], 0.0).then_inc(zero_ready, 1)
                dve.wait_ge(c_all_mm, 1)
                for n, (c_all, b_sb) in enumerate(((c1_all, b1_sb), (c2_all, b2_sb))):
                    for c in range(C):
                        a = dve.tensor_scalar(c_all[:, c, :], bank[n][:, c * NTYPES:(c + 1) * NTYPES],
                                              b_sb[:, c:c + 1], None, ALU.add)
                a.then_inc(c_all_ready, 1)
                dve.wait_ge(c_all_ready, 1)
                dve.tensor_tensor(c12_all[:], c1_all[:], c2_all[:], ALU.mult).then_inc(c12_ready, 1)
                dve.wait_ge(tables_mm, 1)
                for c in range(C):
                    dve.tensor_copy(u_all[:, c, :], bank[2][:, c * NTYPES:(c + 1) * NTYPES])
                    dve.tensor_copy(r_all[:, c, :], bank[3][:, c * NTYPES:(c + 1) * NTYPES])
                dve.tensor_copy(k_all[:], bank[4][:, 0:NTYPES]).then_inc(tables_ready, 1)
                dve.wait_ge(tables_ready, 1)
                dve.wait_ge(zero_ready, 1)
                dve.wait_ge(kinds_ready, 1)

                def spread(row):
                    return row.rearrange("p (o t) -> p o t", o=1).to_broadcast([P, NODES, NTYPES])

                with dve.Fori(0, TOKENS // P) as n:
                    dve.wait_ge(pair_x_mm, n + 1)
                    for c in range(C):
                        dve.tensor_copy(gt_sb[:, c, 0:P], bank[0][:, c * P:(c + 1) * P])
                    dve.tensor_copy(hg_sb[:, 0, 0, 0:HID], bank[1][:, 0:HID])
                    dve.tensor_copy(xr_sb[:], bank[3][:, 0:NTYPES])
                    dve.tensor_tensor(xu_sb[:], bank[2][:, 0:NTYPES], k_all[:], ALU.add).then_inc(pair_x_ready, 1)
                    dve.wait_ge(pair_adj_loaded, 32 * (n + 1))
                    for side, row in ((1, xr_sb), (0, xu_sb)):
                        done = 6 * n + (0 if side else 3)
                        if not side:
                            dve.wait_ge(pair_pick, done)
                        dve.tensor_tensor(onehot[:], adj_sb[:, side, 0, :].rearrange("p (m o) -> p m o", o=1)
                                          .to_broadcast([P, NODES, NTYPES]), spread(kinds[:]),
                                          ALU.is_equal).then_inc(pair_pick, 1)
                        dve.wait_ge(pair_x_ready, n + 1)
                        dve.wait_ge(pair_pick, done + 1)
                        dve.tensor_tensor(onehot[:], onehot[:], spread(row[:]), ALU.mult).then_inc(pair_pick, 1)
                        dve.wait_ge(pair_pick, done + 2)
                        if side:
                            for h in range(2):
                                ps = slice(h * NODES, (h + 1) * NODES)
                                a = dve.tensor_reduce(pick_r[ps, ps], onehot[ps], AX_X, ALU.add)
                        else:
                            a = dve.tensor_reduce(pick_u[:], onehot[:], AX_X, ALU.add)
                        a.then_inc(pair_pick, 1)
                    dve.wait_ge(pair_score_mm, n + 1)
                    dve.wait_ge(pair_pick, 6 * (n + 1))
                    for h in range(2):
                        ps = slice(h * NODES, (h + 1) * NODES)
                        a = dve.tensor_tensor(rel[ps, 0, :], score[ps, ps], pick_u[ps], ALU.add)
                    a.then_inc(pair_rel, 1)
                    dve.tensor_scalar(edges[:], adj_sb[:, 0, 0, :], 0, None, ALU.not_equal).then_inc(pair_rel, 1)
                    dve.wait_ge(pair_rel, 5 * n + 2)
                    dve.tensor_scalar(neg_sb[:, 0, 0, :], edges[:], NEG, -NEG, ALU.mult, ALU.add)
                    dve.tensor_tensor(rel[:, 0, :], rel[:, 0, :], edges[:], ALU.mult).then_inc(pair_rel, 1)
                    dve.wait_ge(pair_rel, 5 * n + 3)
                    dve.tensor_tensor(rel[:, 0, :], rel[:, 0, :], neg_sb[:, 0, 0, :], ALU.add).then_inc(pair_rel, 1)
                    dve.wait_ge(pair_rel, 5 * n + 4)
                    dve.tensor_reduce(nmax[:, 0:1], rel[:, 0, :], AX_X, ALU.max, negate=True).then_inc(pair_rel, 1)
                    dve.wait_ge(pair_exp, n + 1)
                    dve.reciprocal(rsum[:, 0:1], psum_row[:, 0:1]).then_inc(pair_rsum, 1)
                    dve.wait_ge(pair_rsum, n + 1)
                    for h in range(2):
                        ps = slice(h * NODES, (h + 1) * NODES)
                        a = dve.tensor_tensor(attn[ps, 0, ps], prob[ps, 0, :],
                                              rsum[ps, 0:1].to_broadcast([NODES, NODES]), ALU.mult)
                    a.then_inc(pair_attn, 1)
                    dve.wait_ge(pair_out_mm, n + 1)
                    dve.wait_ge(pair_x_loaded, 16 * (n + 1))
                    dve.tensor_tensor(y_sb[:, 0, 0, :], bank[5][:, 0:HID], x_sb[:, 0, 0, :],
                                      ALU.add).then_inc(pair_y, 1)
                    dve.wait_ge(pair_y, 3 * n + 1)
                    dve.tensor_tensor(y_sb[:, 0, 0, :], y_sb[:, 0, 0, :], wob_sb[:], ALU.add).then_inc(pair_y, 1)
                    dve.wait_ge(pair_y, 3 * n + 2)
                    dve.bn_stats(stats[:, 0, :], y_sb[:, 0, 0, :]).then_inc(pair_y, 1)
                    dve.wait_ge(pair_y, 3 * (n + 1))
                    dve.tensor_copy(stats[:, 1, :], stats[:, 0, :])
                    dve.bn_aggr(mv[:, 0, :], stats[:, 0, :]).then_inc(pair_aggr, 1)
                    dve.wait_ge(pair_rstd, n + 1)
                    dve.tensor_scalar(y_sb[:, 0, 0, :], y_sb[:, 0, 0, :], mv[:, 0, 0:1], rstd[:, 0:1],
                                      ALU.subtract, ALU.mult).then_inc(pair_y_ready, 1)

        @block.gpsimd
        def _(pool):
            def split_x(g, slot):
                pool.wait_ge(xhi, g + 1)
                pool.wait_ge(adj_loaded[slot], 16 * (half(g, slot) + 1))
                if not isinstance(g, int) or g > 1:
                    pool.wait_ge(masked, 3 * (g - 1))
                pool.tensor_tensor(xt_lo[:, slot], xt_sb[:, slot], f32(xt_hi[:, slot]),
                                   ALU.subtract).then_inc(xlo, 1)

            def mask(g, slot):
                pool.tensor_scalar(neg_sb[:, slot], adj_sb[:, slot], NEG, -NEG, ALU.mult, ALU.add).then_inc(negm, 1)

            def bias_x(g, slot):
                pool.wait_ge(x_loaded[slot], 16 * (half(g, slot) + 1))
                pool.tensor_tensor(x_sb[:, slot], x_sb[:, slot],
                                   wob_sb[:].rearrange("p (o n) -> p o n", o=1).to_broadcast([P, PAIRS, HID]),
                                   ALU.add).then_inc(xb, 1)

            def inverse_std(g, part, qs):
                n = HALVES * g + part + 1
                pool.wait_ge(aggrd, n)
                pool.tensor_tensor(veps[:, qs], mv[:, qs, 1], eps_sb[:, qs], ALU.add).then_inc(veps_ready, 1)
                pool.wait_ge(veps_ready, n)
                pool.tensor_tensor(rstd[:, qs], veps[:, qs], mhalf[:, qs], ALU.pow).then_inc(rstd_ready, 1)

            def shift(g, part, pairs):
                pool.wait_ge(rstd_ready, HALVES * g + part + 1)
                for q in pairs:
                    a = pool.tensor_scalar(nmr[:, q:q + 1], mv[:, q, 0:1], rstd[:, q:q + 1], -1.0, ALU.mult, ALU.mult)
                a.then_inc(nmr_ready, 1)

            pool.memset(mhalf[:], -0.5)
            pool.memset(eps_sb[:], EPS)
            pool.iota(kinds[:], pattern=[[1, NTYPES]], base=0, channel_multiplier=0).then_inc(kinds_ready, 1)
            pool.memset(ident[:], 0.0).then_inc(ident_zero, 1)
            pool.wait_ge(ident_zero, 1)
            pool.affine_select(out=ident[:], in_=ident[:], compare_op=ALU.not_equal, fill=1.0, base=0,
                               pattern=[[-1, P]], channel_multiplier=1).then_inc(ident_ready, 1)
            pool.wait_ge(adj_loaded[0], 16)
            mask(0, 0)
            pool.wait_ge(xlo, 1)
            split_x(1, 1)
            mask(1, 1)
            pool.wait_ge(wob_loaded, 16)
            bias_x(0, 0)

            def body(g, par, first, last):
                if not first and not last:
                    split_x(g + 1, 1 - par)
                    mask(g + 1, 1 - par)
                if not first:
                    for h in range(HALVES):
                        inverse_std(g - 1, h, slice(2 * h, 2 * h + 2))
                        if last:
                            shift(g - 1, h, (2 * h, 2 * h + 1))
                if not last:
                    bias_x(g + 1, 1 - par)
                for f in ((1,) if last else (0, 2)):
                    pool.wait_ge(hshi, C * g + f + 1)
                    pool.tensor_tensor(hs_lo[:, f, :], hs_sb[:, f, :], f32(hs_hi[:, f, :]),
                                       ALU.subtract).then_inc(hslo1 if last else hslo, 1)

            run(pool, body)
            pool.wait_ge(y_end, HALVES)
            for q in (0, 1):
                inverse_std(GROUPS - 1, q, slice(q, q + 1))
                shift(GROUPS - 1, q, (q,))
            inverse_std(GROUPS - 1, 2, slice(2, 4))

            with pool.If(is_general(pool)):
                with pool.Fori(0, TOKENS // P) as n:
                    pool.wait_ge(pair_aggr, n + 1)
                    pool.tensor_tensor(veps[:, 0:1], mv[:, 0, 1:2], eps_sb[:, 0:1], ALU.add).then_inc(pair_veps, 1)
                    pool.wait_ge(pair_veps, n + 1)
                    pool.tensor_tensor(rstd[:, 0:1], veps[:, 0:1], mhalf[:, 0:1], ALU.pow).then_inc(pair_rstd, 1)


def kernel(x, adj, L0_gnn_dep_emb_table, L0_gnn_W1_w, L0_gnn_W1_b, L0_gnn_W2_w, L0_gnn_W2_b,
           L0_gnn_gcn_w, L0_gnn_gcn_b, L0_gnn_Wo_w, L0_gnn_Wo_b):
    import numpy as np
    import concourse.bacc as bacc
    from concourse.bass_utils import run_bass_kernel_spmd

    x = np.asarray(x)
    hid = x.shape[2]
    w1, w2 = np.asarray(L0_gnn_W1_w), np.asarray(L0_gnn_W2_w)

    def columns(b):
        return np.asarray(b).reshape(-1, P).T

    laid_out = {
        "x": x,
        "x_t": x.reshape(-1, hid).T,
        "adj": np.asarray(adj),
        "adj_t": np.asarray(adj).transpose(0, 2, 1),
        "edge": np.concatenate([np.asarray(L0_gnn_dep_emb_table).T, w1[hid:], w2[hid:]], axis=1),
        "biases": np.concatenate([columns(b) for b in (L0_gnn_W1_b, L0_gnn_W2_b, L0_gnn_gcn_b)], axis=1),
        "w1_t": w1[:hid].T,
        "w2_t": w2[:hid].T,
        "gcn_w": np.asarray(L0_gnn_gcn_w),
        "wo_w": np.asarray(L0_gnn_Wo_w),
        "wo_b": np.asarray(L0_gnn_Wo_b).reshape(1, hid),
    }
    nc = bacc.Bacc("TRN2", target_bir_lowering=False, num_devices=1)
    arrays, args = {}, []
    for name, a in laid_out.items():
        a = np.ascontiguousarray(a)
        arrays[f"in_{name}_dram"] = a
        args.append(nc.dram_tensor(f"in_{name}_dram", a.shape, mybir.dt.from_np(a.dtype), kind="ExternalInput").ap())
    out = nc.dram_tensor("out_0_dram", x.shape, F32, kind="ExternalOutput").ap()
    gnn_layernorm_kernel(nc, *args, out)
    result = run_bass_kernel_spmd(nc, [arrays], core_ids=[0])
    return result.results[0]["out_0_dram"]
```
